# Optimizing a Trainium2 kernel written in Bass

```python
import numpy as np
import jax
import jax.numpy as jnp

def _softmax(x, axis=-1):
    return jax.nn.softmax(x, axis=axis)

def _gelu(x):
    return jax.nn.gelu(x, approximate=True)

def _silu(x):
    return jax.nn.silu(x)

def _sigmoid(x):
    return jax.nn.sigmoid(x)

def _layernorm(x, axis=-1, eps=1e-05):
    m = jnp.mean(x, axis=axis, keepdims=True)
    v = jnp.var(x, axis=axis, keepdims=True)
    return (x - m) / jnp.sqrt(v + eps)

def _scatter_add(tgt, idx, src, axis=0):
    return tgt.at[idx].add(src)

def _segment_sum(src, seg, n):
    return jax.ops.segment_sum(src, seg, n)
kernel_name = 'mk_perceiver_d2_seqx_r4_c136fa'

def setup_inputs(seed: int=0):
    np.random.seed(seed)
    _w = jnp.asarray

    def _rec_inputs():
        import jax
        import jax.numpy as jnp
        _rk = jax.random.key(seed)
        x = -0.0002928 + 1 * jax.random.normal(jax.random.fold_in(_rk, 1), (64, 32, 256), jnp.float32)
        _lenS = 32 - jax.random.randint(jax.random.fold_in(_rk, 7), (64,), 0, max(1, 32 // 4) + 1, jnp.int32)
        _lenS2 = 257 - jax.random.randint(jax.random.fold_in(_rk, 8), (64,), 0, max(1, 257 // 4) + 1, jnp.int32)
        _ctx_1024P = jax.random.normal(jax.random.fold_in(_rk, 11), (64, 16, 256), jnp.float32)
        _ctx_1024c = jax.random.dirichlet(jax.random.fold_in(_rk, 511), 0.3 * jnp.ones((16,), jnp.float32), (64, 257))
        _ctx_1024t = jnp.einsum('bsk,bkd->bsd', _ctx_1024c, _ctx_1024P)
        _ctx_1024t = _ctx_1024t * jax.lax.rsqrt(jnp.mean(jnp.square(_ctx_1024t)) + 1e-12) * 0.953939
        ctx_1024 = -1.39393e-06 + 0.999914 * (_ctx_1024t + 0.3 * jax.random.normal(jax.random.fold_in(_rk, 611), (64, 257, 256), jnp.float32))
        return (x, ctx_1024)
    x, ctx_1024 = _rec_inputs()

    def _L0_xattn_setup():
        import jax, jax.numpy as jnp
        import numpy as np
        import math
        D_MODEL = 256
        N_HEADS = 16
        key = jax.random.key(seed)
        ks = jax.random.split(key, 11)
        N, L, S = (2, 512, 512)
        d = D_MODEL
        s = 1.0 / math.sqrt(d)
        return {'queries': jax.random.normal(ks[0], (N, L, d), dtype=jnp.float32), 'keys': jax.random.normal(ks[1], (N, S, d), dtype=jnp.float32), 'values': jax.random.normal(ks[2], (N, S, d), dtype=jnp.float32), 'Wq': jax.random.normal(ks[3], (d, d), dtype=jnp.float32) * s, 'bq': jax.random.normal(ks[4], (d,), dtype=jnp.float32) * s, 'Wk': jax.random.normal(ks[5], (d, d), dtype=jnp.float32) * s, 'bk': jax.random.normal(ks[6], (d,), dtype=jnp.float32) * s, 'Wv': jax.random.normal(ks[7], (d, d), dtype=jnp.float32) * s, 'bv': jax.random.normal(ks[8], (d,), dtype=jnp.float32) * s, 'Wo': jax.random.normal(ks[9], (d, d), dtype=jnp.float32) * s, 'bo': jax.random.normal(ks[10], (d,), dtype=jnp.float32) * s}
    _L0_xattn_all = _L0_xattn_setup()
    _L0_xattn_in = {k: v for k, v in _L0_xattn_all.items() if k in ('Wq', 'bq', 'Wk', 'bk', 'Wv', 'bv', 'Wo', 'bo')}
    del _L0_xattn_all

    def _L0_attn_setup():
        import jax, jax.numpy as jnp
        import numpy as np
        OFFSETS = sorted(set(range(0, 33)) | {48, 64, 96, 128, 192, 64, 96, 128, 192, 256, 384})
        B, N, D, H = (2, 512, 256, 16)
        HD = D // H

        def _shift(t, delta, n):
            if delta == 0:
                return t
            if delta >= n:
                return jnp.zeros_like(t)
            return jnp.pad(t[:, :, :n - delta], ((0, 0), (0, 0), (delta, 0), (0, 0)))
        key = jax.random.key(seed)
        ks = jax.random.split(key, 4)
        x = jax.random.normal(ks[0], (B, N, D), jnp.float32)
        Wqkv = jax.random.normal(ks[1], (D, 3 * D), jnp.float32) * D ** (-0.5)
        bqkv = jnp.zeros((3 * D,), jnp.float32)
        Wout = jax.random.normal(ks[2], (D, D), jnp.float32) * D ** (-0.5)
        bout = jnp.zeros((D,), jnp.float32)
        Wgate = jax.random.normal(ks[3], (D, D), jnp.float32) * D ** (-0.5)
        bgate = jnp.full((D,), 2.0, jnp.float32)
        alphas = np.linspace(0.2, 2.0, H, dtype=np.float32)
        deltas = np.log1p(np.asarray(OFFSETS, dtype=np.float32))
        pos_bias = jnp.asarray(-deltas[:, None] * alphas[None, :], jnp.float32)
        return dict(x=x, Wqkv=Wqkv, bqkv=bqkv, Wout=Wout, bout=bout, Wgate=Wgate, bgate=bgate, pos_bias=pos_bias)
    _L0_attn_all = _L0_attn_setup()
    _L0_attn_in = {k: v for k, v in _L0_attn_all.items() if k in ('Wqkv', 'bqkv', 'Wout', 'bout', 'Wgate', 'bgate', 'pos_bias')}
    del _L0_attn_all

    def _L0_ffn_setup():
        import jax, jax.numpy as jnp
        import numpy as np
        BLOCK = 32
        W_BITS = 4
        ACT_BITS = 16

        def act_qdq(x):
            qmax = 2.0 ** (ACT_BITS - 1) - 1.0
            scale = jnp.maximum(jnp.max(jnp.abs(x)) / qmax, 1e-12)
            return jnp.clip(jnp.round(x / scale), -qmax - 1.0, qmax) * scale

        def fixed_qdq_u16(x):
            scale = 1.0 / 65536.0
            return jnp.clip(jnp.round(x / scale), 0.0, 65535.0) * scale

        def lpbq_dequant(w):
            O, I = w.shape
            qmax = 2.0 ** (W_BITS - 1) - 1.0
            wb = w.reshape(O, I // BLOCK, BLOCK)
            s = jnp.maximum(jnp.max(jnp.abs(wb), axis=-1, keepdims=True) / qmax, 1e-12)
            wq = jnp.clip(jnp.round(wb / s), -qmax - 1.0, qmax) * s
            return wq.reshape(O, I)
        key = jax.random.key(seed)
        k1, k2, k3, k4 = jax.random.split(key, 4)
        B, S, H, I = (2, 1024, 256, 768)
        x = jax.random.normal(k1, (B, S, H), jnp.float32)
        w_gate = jax.random.normal(k2, (I, H), jnp.float32) * 0.02
        w_up = jax.random.normal(k3, (I, H), jnp.float32) * 0.02
        w_down = jax.random.normal(k4, (H, I), jnp.float32) * 0.02
        return {'x': x, 'w_gate': w_gate, 'w_up': w_up, 'w_down': w_down}
    _L0_ffn_all = _L0_ffn_setup()
    _L0_ffn_in = {k: v for k, v in _L0_ffn_all.items() if k in ('w_gate', 'w_up', 'w_down')}
    del _L0_ffn_all

    def _L1_xattn_setup():
        import jax, jax.numpy as jnp
        import numpy as np
        DIM = 256
        N_HEADS = 16
        HEAD_DIM = DIM // N_HEADS
        B, N, M = (2, 512, 512)
        key = jax.random.key(seed)
        ks = jax.random.split(key, 10)
        s = 1.0 / np.sqrt(DIM)
        return {'x1': jax.random.normal(ks[0], (B, N, DIM), dtype=jnp.float32), 'x2': jax.random.normal(ks[1], (B, M, DIM), dtype=jnp.float32), 'Wq': jax.random.normal(ks[2], (DIM, DIM), dtype=jnp.float32) * s, 'bq': jnp.zeros((DIM,), dtype=jnp.float32), 'Wk': jax.random.normal(ks[3], (DIM, DIM), dtype=jnp.float32) * s, 'bk': jnp.zeros((DIM,), dtype=jnp.float32), 'Wv': jax.random.normal(ks[4], (DIM, DIM), dtype=jnp.float32) * s, 'bv': jnp.zeros((DIM,), dtype=jnp.float32), 'Wo': jax.random.normal(ks[5], (DIM, DIM), dtype=jnp.float32) * s, 'bo': jnp.zeros((DIM,), dtype=jnp.float32)}
    _L1_xattn_all = _L1_xattn_setup()
    _L1_xattn_in = {k: v for k, v in _L1_xattn_all.items() if k in ('Wq', 'bq', 'Wk', 'bk', 'Wv', 'bv', 'Wo', 'bo')}
    del _L1_xattn_all

    def _L1_attn_setup():
        import jax, jax.numpy as jnp
        import numpy as np
        _J6 = jnp.array([[0, 0, 0, 0, 0, 1], [0, 0, 0, 0, -1, 0], [0, 0, 0, 1, 0, 0], [0, 0, 1, 0, 0, 0], [0, -1, 0, 0, 0, 0], [1, 0, 0, 0, 0, 0]], dtype=jnp.float32)
        _PI = np.array([0, 0, 0, 1, 1, 2])
        _PJ = np.array([1, 2, 3, 2, 3, 3])

        def plucker_lines(p1, p2):
            lines = p1[..., _PI] * p2[..., _PJ] - p1[..., _PJ] * p2[..., _PI]
            n = jnp.linalg.norm(lines, axis=-1, keepdims=True)
            return lines / jnp.maximum(n, 1e-12)
        key = jax.random.key(seed)
        ks = jax.random.split(key, 6)
        B, T, D, H = (1, 512, 256, 16)
        s = D ** (-0.5)
        x = jax.random.normal(ks[0], (B, T, D), jnp.float32)
        Wqkv = jax.random.normal(ks[1], (D, 3 * D), jnp.float32) * s
        bqkv = jnp.zeros((3 * D,), jnp.float32)
        W1p = jax.random.normal(ks[2], (D, 4 * H), jnp.float32) * s
        W2p = jax.random.normal(ks[3], (D, 4 * H), jnp.float32) * s
        plucker_scale = jnp.full((H,), 0.1, jnp.float32)
        Wout = jax.random.normal(ks[4], (D, D), jnp.float32) * s
        bout = jnp.zeros((D,), jnp.float32)
        return {'x': x, 'Wqkv': Wqkv, 'bqkv': bqkv, 'W1p': W1p, 'W2p': W2p, 'plucker_scale': plucker_scale, 'Wout': Wout, 'bout': bout}
    _L1_attn_all = _L1_attn_setup()
    _L1_attn_in = {k: v for k, v in _L1_attn_all.items() if k in ('Wqkv', 'bqkv', 'W1p', 'W2p', 'plucker_scale', 'Wout', 'bout')}
    del _L1_attn_all

    def _L1_ffn_setup():
        import jax, jax.numpy as jnp
        import numpy as np
        D_IN, D_HID = (256, 1024)

        def _ternary(key, shape):
            return jax.random.randint(key, shape, -1, 2).astype(jnp.float32)

        def _tlin(x, w, s):
            return jnp.einsum('bsi,oi->bso', x, w) * s
        key = jax.random.key(seed)
        ks = jax.random.split(key, 12)
        inv = lambda fan: 1.0 / np.sqrt(fan).astype(np.float32)
        return {'x': jax.random.normal(ks[0], (4, 512, D_IN), dtype=jnp.float32), 'w1_w': _ternary(ks[1], (D_HID, D_IN)), 'w1_s': jax.random.uniform(ks[2], (D_HID,), dtype=jnp.float32) * inv(D_IN), 'w2_w': _ternary(ks[3], (D_HID, D_IN)), 'w2_s': jax.random.uniform(ks[4], (D_HID,), dtype=jnp.float32) * inv(D_IN), 'h1_w': _ternary(ks[5], (D_HID, D_HID)), 'h1_s': jax.random.uniform(ks[6], (D_HID,), dtype=jnp.float32) * inv(D_HID), 'h2_w': _ternary(ks[7], (D_HID, D_HID)), 'h2_s': jax.random.uniform(ks[8], (D_HID,), dtype=jnp.float32) * inv(D_HID), 'w3_w': _ternary(ks[9], (D_IN, D_HID)), 'w3_s': jax.random.uniform(ks[10], (D_IN,), dtype=jnp.float32) * inv(D_HID)}
    _L1_ffn_all = _L1_ffn_setup()
    _L1_ffn_in = {k: v for k, v in _L1_ffn_all.items() if k in ('w1_w', 'w1_s', 'w2_w', 'w2_s', 'h1_w', 'h1_s', 'h2_w', 'h2_s', 'w3_w', 'w3_s')}
    del _L1_ffn_all
    return {'x': x, 'ctx_1024': ctx_1024, 'L0_xattn_Wq': _L0_xattn_in['Wq'], 'L0_xattn_bq': _L0_xattn_in['bq'], 'L0_xattn_Wk': _L0_xattn_in['Wk'], 'L0_xattn_bk': _L0_xattn_in['bk'], 'L0_xattn_Wv': _L0_xattn_in['Wv'], 'L0_xattn_bv': _L0_xattn_in['bv'], 'L0_xattn_Wo': _L0_xattn_in['Wo'], 'L0_xattn_bo': _L0_xattn_in['bo'], 'L0_attn_Wqkv': _L0_attn_in['Wqkv'], 'L0_attn_bqkv': _L0_attn_in['bqkv'], 'L0_attn_Wout': _L0_attn_in['Wout'], 'L0_attn_bout': _L0_attn_in['bout'], 'L0_attn_Wgate': _L0_attn_in['Wgate'], 'L0_attn_bgate': _L0_attn_in['bgate'], 'L0_attn_pos_bias': _L0_attn_in['pos_bias'], 'L0_ffn_w_gate': _L0_ffn_in['w_gate'], 'L0_ffn_w_up': _L0_ffn_in['w_up'], 'L0_ffn_w_down': _L0_ffn_in['w_down'], 'L1_xattn_Wq': _L1_xattn_in['Wq'], 'L1_xattn_bq': _L1_xattn_in['bq'], 'L1_xattn_Wk': _L1_xattn_in['Wk'], 'L1_xattn_bk': _L1_xattn_in['bk'], 'L1_xattn_Wv': _L1_xattn_in['Wv'], 'L1_xattn_bv': _L1_xattn_in['bv'], 'L1_xattn_Wo': _L1_xattn_in['Wo'], 'L1_xattn_bo': _L1_xattn_in['bo'], 'L1_attn_Wqkv': _L1_attn_in['Wqkv'], 'L1_attn_bqkv': _L1_attn_in['bqkv'], 'L1_attn_W1p': _L1_attn_in['W1p'], 'L1_attn_W2p': _L1_attn_in['W2p'], 'L1_attn_plucker_scale': _L1_attn_in['plucker_scale'], 'L1_attn_Wout': _L1_attn_in['Wout'], 'L1_attn_bout': _L1_attn_in['bout'], 'L1_ffn_w1_w': _L1_ffn_in['w1_w'], 'L1_ffn_w1_s': _L1_ffn_in['w1_s'], 'L1_ffn_w2_w': _L1_ffn_in['w2_w'], 'L1_ffn_w2_s': _L1_ffn_in['w2_s'], 'L1_ffn_h1_w': _L1_ffn_in['h1_w'], 'L1_ffn_h1_s': _L1_ffn_in['h1_s'], 'L1_ffn_h2_w': _L1_ffn_in['h2_w'], 'L1_ffn_h2_s': _L1_ffn_in['h2_s'], 'L1_ffn_w3_w': _L1_ffn_in['w3_w'], 'L1_ffn_w3_s': _L1_ffn_in['w3_s']}

def reference(x, ctx_1024, L0_xattn_Wq, L0_xattn_bq, L0_xattn_Wk, L0_xattn_bk, L0_xattn_Wv, L0_xattn_bv, L0_xattn_Wo, L0_xattn_bo, L0_attn_Wqkv, L0_attn_bqkv, L0_attn_Wout, L0_attn_bout, L0_attn_Wgate, L0_attn_bgate, L0_attn_pos_bias, L0_ffn_w_gate, L0_ffn_w_up, L0_ffn_w_down, L1_xattn_Wq, L1_xattn_bq, L1_xattn_Wk, L1_xattn_bk, L1_xattn_Wv, L1_xattn_bv, L1_xattn_Wo, L1_xattn_bo, L1_attn_Wqkv, L1_attn_bqkv, L1_attn_W1p, L1_attn_W2p, L1_attn_plucker_scale, L1_attn_Wout, L1_attn_bout, L1_ffn_w1_w, L1_ffn_w1_s, L1_ffn_w2_w, L1_ffn_w2_s, L1_ffn_h1_w, L1_ffn_h1_s, L1_ffn_h2_w, L1_ffn_h2_s, L1_ffn_w3_w, L1_ffn_w3_s):
    import jax
    import jax.numpy as jnp

    def _L0_xattn_ref(queries, keys, values, Wq, bq, Wk, bk, Wv, bv, Wo, bo):
        import jax, jax.numpy as jnp
        import numpy as np
        import math
        D_MODEL = 256
        N_HEADS = 16
        N, L, _ = queries.shape
        S = keys.shape[1]
        H = N_HEADS
        q = (queries @ Wq.T + bq).reshape(N, L, H, -1)
        k = (keys @ Wk.T + bk).reshape(N, S, H, -1)
        v = (values @ Wv.T + bv).reshape(N, S, H, -1)
        D = k.shape[-1]
        sm = jnp.einsum('nlhd,nshd->nlhs', q, k) / math.sqrt(D)
        causal_mask = jnp.triu(jnp.ones((L, S), dtype=bool), k=1)
        sm = jnp.where(causal_mask[None, :, None, :], -jnp.inf, sm)
        sm = jax.nn.softmax(sm, axis=-1)
        attn = jnp.einsum('nlhs,nshd->nlhd', sm, v)
        new_values = attn.reshape(N, L, H * D)
        return new_values @ Wo.T + bo

    def _L0_attn_ref(x, Wqkv, bqkv, Wout, bout, Wgate, bgate, pos_bias):
        import jax, jax.numpy as jnp
        import numpy as np
        OFFSETS = sorted(set(range(0, 33)) | {48, 64, 96, 128, 192, 64, 96, 128, 192, 256, 384})
        B, N, D, H = (2, 512, 256, 16)
        HD = D // H

        def _shift(t, delta, n):
            if delta == 0:
                return t
            if delta >= n:
                return jnp.zeros_like(t)
            return jnp.pad(t[:, :, :n - delta], ((0, 0), (0, 0), (delta, 0), (0, 0)))
        b, n, d = x.shape
        scale = HD ** (-0.5)
        qkv = x @ Wqkv + bqkv
        q, k, v = jnp.split(qkv, 3, axis=-1)
        q = q.reshape(b, n, H, HD).transpose(0, 2, 1, 3)
        k = k.reshape(b, n, H, HD).transpose(0, 2, 1, 3)
        v = v.reshape(b, n, H, HD).transpose(0, 2, 1, 3)
        scores = jnp.stack([jnp.einsum('bhnd,bhnd->bhn', q, _shift(k, delta, n)) for delta in OFFSETS], axis=-1) * scale
        scores = scores + pos_bias.T[None, :, None, :]
        invalid = jnp.arange(n)[:, None] < jnp.asarray(OFFSETS)[None, :]
        scores = jnp.where(invalid[None, None], -jnp.inf, scores)
        alpha = jax.nn.softmax(scores, axis=-1)
        out = jnp.zeros_like(q)
        for i, delta in enumerate(OFFSETS):
            out = out + alpha[..., i:i + 1] * _shift(v, delta, n)
        flat = out.transpose(0, 2, 1, 3).reshape(b, n, d)
        gate = jax.nn.sigmoid(x @ Wgate + bgate)
        return flat * gate @ Wout + bout

    def _L0_ffn_ref(x, w_gate, w_up, w_down):
        import jax, jax.numpy as jnp
        import numpy as np
        BLOCK = 32
        W_BITS = 4
        ACT_BITS = 16

        def act_qdq(x):
            qmax = 2.0 ** (ACT_BITS - 1) - 1.0
            scale = jnp.maximum(jnp.max(jnp.abs(x)) / qmax, 1e-12)
            return jnp.clip(jnp.round(x / scale), -qmax - 1.0, qmax) * scale

        def fixed_qdq_u16(x):
            scale = 1.0 / 65536.0
            return jnp.clip(jnp.round(x / scale), 0.0, 65535.0) * scale

        def lpbq_dequant(w):
            O, I = w.shape
            qmax = 2.0 ** (W_BITS - 1) - 1.0
            wb = w.reshape(O, I // BLOCK, BLOCK)
            s = jnp.maximum(jnp.max(jnp.abs(wb), axis=-1, keepdims=True) / qmax, 1e-12)
            wq = jnp.clip(jnp.round(wb / s), -qmax - 1.0, qmax) * s
            return wq.reshape(O, I)
        x = act_qdq(x)
        up = act_qdq(x @ lpbq_dequant(w_up).T)
        gate = act_qdq(x @ lpbq_dequant(w_gate).T)
        sig = fixed_qdq_u16(jax.nn.sigmoid(gate))
        gate = act_qdq(gate * sig)
        o = act_qdq(gate * up)
        return o @ lpbq_dequant(w_down).T

    def _L1_xattn_ref(x1, x2, Wq, bq, Wk, bk, Wv, bv, Wo, bo):
        import jax, jax.numpy as jnp
        import numpy as np
        DIM = 256
        N_HEADS = 16
        HEAD_DIM = DIM // N_HEADS
        B, N, M = (2, 512, 512)
        b, n, _ = x1.shape
        m = x2.shape[1]
        q = x1 @ Wq.T + bq
        k = x2 @ Wk.T + bk
        v = x2 @ Wv.T + bv
        q = q.reshape(b, n, N_HEADS, HEAD_DIM).transpose(0, 2, 1, 3)
        k = k.reshape(b, m, N_HEADS, HEAD_DIM).transpose(0, 2, 1, 3)
        v = v.reshape(b, m, N_HEADS, HEAD_DIM).transpose(0, 2, 1, 3)
        scale = 1.0 / jnp.sqrt(jnp.asarray(HEAD_DIM, dtype=q.dtype))
        scores = jnp.einsum('bhnd,bhmd->bhnm', q, k) * scale
        attn = jax.nn.softmax(scores, axis=-1)
        o = jnp.einsum('bhnm,bhmd->bhnd', attn, v)
        o = o.transpose(0, 2, 1, 3).reshape(b, n, DIM)
        return o @ Wo.T + bo

    def _L1_attn_ref(x, Wqkv, bqkv, W1p, W2p, plucker_scale, Wout, bout):
        import jax, jax.numpy as jnp
        import numpy as np
        _J6 = jnp.array([[0, 0, 0, 0, 0, 1], [0, 0, 0, 0, -1, 0], [0, 0, 0, 1, 0, 0], [0, 0, 1, 0, 0, 0], [0, -1, 0, 0, 0, 0], [1, 0, 0, 0, 0, 0]], dtype=jnp.float32)
        _PI = np.array([0, 0, 0, 1, 1, 2])
        _PJ = np.array([1, 2, 3, 2, 3, 3])

        def plucker_lines(p1, p2):
            lines = p1[..., _PI] * p2[..., _PJ] - p1[..., _PJ] * p2[..., _PI]
            n = jnp.linalg.norm(lines, axis=-1, keepdims=True)
            return lines / jnp.maximum(n, 1e-12)
        B, T, D = x.shape
        H = plucker_scale.shape[0]
        dh = D // H
        qkv = (x @ Wqkv + bqkv).reshape(B, T, 3, H, dh)
        q = jnp.transpose(qkv[:, :, 0], (0, 2, 1, 3))
        k = jnp.transpose(qkv[:, :, 1], (0, 2, 1, 3))
        v = jnp.transpose(qkv[:, :, 2], (0, 2, 1, 3))
        std_logits = jnp.einsum('bhid,bhjd->bhij', q, k) * dh ** (-0.5)
        p1 = (x @ W1p).reshape(B, T, H, 4)
        p2 = (x @ W2p).reshape(B, T, H, 4)
        lines_h = jnp.transpose(plucker_lines(p1, p2), (0, 2, 1, 3))
        Jlines = lines_h @ _J6.T
        plucker_bias = jnp.einsum('bhic,bhjc->bhij', lines_h, Jlines)
        logits = std_logits + plucker_bias * plucker_scale[None, :, None, None]
        causal = jnp.triu(jnp.ones((T, T), bool), 1)
        logits = jnp.where(causal[None, None], -jnp.inf, logits)
        attn = jax.nn.softmax(logits, axis=-1)
        out = jnp.einsum('bhij,bhjd->bhid', attn, v)
        out = jnp.transpose(out, (0, 2, 1, 3)).reshape(B, T, D)
        return out @ Wout + bout

    def _L1_ffn_ref(x, w1_w, w1_s, w2_w, w2_s, h1_w, h1_s, h2_w, h2_s, w3_w, w3_s):
        import jax, jax.numpy as jnp
        import numpy as np
        D_IN, D_HID = (256, 1024)

        def _ternary(key, shape):
            return jax.random.randint(key, shape, -1, 2).astype(jnp.float32)

        def _tlin(x, w, s):
            return jnp.einsum('bsi,oi->bso', x, w) * s
        h = jax.nn.silu(_tlin(x, w1_w, w1_s)) * _tlin(x, w2_w, w2_s)
        h = jax.nn.gelu(_tlin(h, h1_w, h1_s), approximate=False)
        h = jax.nn.gelu(_tlin(h, h2_w, h2_s), approximate=False)
        return _tlin(h, w3_w, w3_s)
    x = x + _L0_xattn_ref(_layernorm(x, axis=-1), ctx_1024, ctx_1024, L0_xattn_Wq, L0_xattn_bq, L0_xattn_Wk, L0_xattn_bk, L0_xattn_Wv, L0_xattn_bv, L0_xattn_Wo, L0_xattn_bo)
    x = x + _L0_attn_ref(_layernorm(x, axis=-1), L0_attn_Wqkv, L0_attn_bqkv, L0_attn_Wout, L0_attn_bout, L0_attn_Wgate, L0_attn_bgate, L0_attn_pos_bias)
    x = x + _L0_ffn_ref(_layernorm(x, axis=-1), L0_ffn_w_gate, L0_ffn_w_up, L0_ffn_w_down)
    x = x + _L1_xattn_ref(_layernorm(x, axis=-1), ctx_1024, L1_xattn_Wq, L1_xattn_bq, L1_xattn_Wk, L1_xattn_bk, L1_xattn_Wv, L1_xattn_bv, L1_xattn_Wo, L1_xattn_bo)
    x = x + _L1_attn_ref(_layernorm(x, axis=-1), L1_attn_Wqkv, L1_attn_bqkv, L1_attn_W1p, L1_attn_W2p, L1_attn_plucker_scale, L1_attn_Wout, L1_attn_bout)
    x = x + _L1_ffn_ref(_layernorm(x, axis=-1), L1_ffn_w1_w, L1_ffn_w1_s, L1_ffn_w2_w, L1_ffn_w2_s, L1_ffn_h1_w, L1_ffn_h1_s, L1_ffn_h2_w, L1_ffn_h2_s, L1_ffn_w3_w, L1_ffn_w3_s)
    return x

_drawn_inputs = setup_inputs


def setup_inputs(seed=0):
    import zlib

    import numpy as np

    out = dict(_drawn_inputs(seed))
    spreads = {'L0_attn_bqkv': (0.0, 0.1),
     'L0_attn_bout': (0.0, 0.1),
     'L0_attn_bgate': (2.0, 0.2),
     'L1_xattn_bq': (0.0, 0.1),
     'L1_xattn_bk': (0.0, 0.1),
     'L1_xattn_bv': (0.0, 0.1),
     'L1_xattn_bo': (0.0, 0.1),
     'L1_attn_bqkv': (0.0, 0.1),
     'L1_attn_plucker_scale': (0.10000000149011612, 0.2),
     'L1_attn_bout': (0.0, 0.1)}
    factors = {}
    for name, (base, spread) in spreads.items():
        noise = np.random.default_rng([zlib.crc32(name.encode()), seed]).standard_normal(out[name].shape)
        drawn = base * np.exp(spread * noise) if base else spread * noise
        out[name] = jnp.asarray(drawn.astype(out[name].dtype))
    for name, factor in factors.items():
        out[name] = (out[name] * factor).astype(out[name].dtype)
    return out
```

```python
import concourse.bass as bass
from concourse import mybir
from contextlib import ExitStack

F32 = mybir.dt.float32
ALU = mybir.AluOpType
ACT = mybir.ActivationFunctionType
AX = mybir.AxisListType

P = 128
D = 256
KI = D // P
NSEQ = 64
L = 32
S = 257
T = NSEQ * L // P
SPT = P // L
H = 16
HD = D // H
G = 4
J = H // G
NL = 2
NT = T // NL
F0 = 768
NF0 = F0 // P
F1 = 1024
NF1 = F1 // P
BLK = 512
NB = NSEQ * L // BLK
TPB = BLK // P
EPS = 1e-5
MAGIC = 12582912.0
QMAX = 32767.0
NLINE = 6
SLOT = 32


def perceiver(nc, A, out):
    ctx = ExitStack()
    with ctx:
        def sb(name, shape, dt=F32):
            return ctx.enter_context(nc.sbuf_tensor(name, shape, dt))

        def sem(name):
            return ctx.enter_context(nc.semaphore(name))

        def lanes(name):
            return [sem(f"{name}{l}") for l in range(NL)]

        x = sb("x", [P, T, D])
        ident = sb("ident", [P, P])
        sel = sb("sel", [P, L])
        mask8 = sb("mask8", [P, 8])
        mask4 = sb("mask4", [P, 4])
        causal = sb("causal", [P, H * L])
        posmask = sb("posmask", [P, H * L])
        minus_half = sb("minus_half", [P, H])
        x1_wq, x1_wk, x1_wv, x1_wo = (sb(f"x1_w{c}", [P, KI, D]) for c in "qkvo")
        a1_wqkv = sb("a1_wqkv", [P, KI, 3 * D])
        a1_wpl = sb("a1_wpl", [P, KI, 2, 4 * H])
        a1_wout = sb("a1_wout", [P, KI, D])
        colb = sb("colb", [P, 10, KI])
        BQ0, BK0, BV0, BQA, BKA, BVA, BG, BQ1, BK1, BV1 = range(10)
        a1_bv = sb("a1_bv", [P, KI])
        nbg = sb("nbg", [P, KI])
        rowb = sb("rowb", [P, 4, D])
        BO0, BOA, BO1, BOB = range(4)
        a1_bqk = sb("a1_bqk", [P, 2 * D])
        plsc = sb("plsc", [P, H, NLINE])
        plscale = sb("plscale", [P, H])
        plsign = sb("plsign", [P, NLINE])
        ffn_s = sb("ffn_s", [P, 4, NF1])
        w3s = sb("w3s", [P, D])

        LANE = 8448
        R1 = NL * LANE
        RSIZE = R1 + 2 * KI * F1 + 2 * NF1 * F1 + NF1 * D
        R = sb("R", [P, RSIZE])

        def view(at, *shape):
            size = 1
            for s in shape:
                size *= s
            assert at + size <= RSIZE
            v = R[:, at:at + size]
            if len(shape) == 2:
                v = v.rearrange("p (a b) -> p a b", b=shape[1])
            elif len(shape) == 3:
                v = v.rearrange("p (a b c) -> p a b c", b=shape[1], c=shape[2])
            elif len(shape) == 4:
                v = v.rearrange("p (a b c d) -> p a b c d", b=shape[1], c=shape[2], d=shape[3])
            return v

        def put(at, sizes):
            places = []
            for s in sizes:
                places.append(at)
                at += s
            return places

        lane_at = [put(l * LANE, [256, 256, 2048, 512, 1024, 512, 512, 512, 1024, 256, 256, 512, 512, 256])
                   for l in range(NL)]
        xn = [view(a[0], D) for a in lane_at]
        xnT = [view(a[1], KI, P) for a in lane_at]
        qbd = [view(a[2], 2048) for a in lane_at]
        kT = [view(a[3], 512) for a in lane_at]
        vbd = [view(a[4], SPT, D) for a in lane_at]
        sc = [view(a[5], H, L) for a in lane_at]
        pr = [view(a[6], G, P) for a in lane_at]
        pT = [view(a[7], G, P) for a in lane_at]
        om = [view(a[8], KI * SPT * P) for a in lane_at]
        oT = [view(a[9], KI, P) for a in lane_at]
        gT = [view(a[10], KI, P) for a in lane_at]
        qs = [view(a[11], H, SLOT) for a in lane_at]
        qT = [view(a[11], D) for a in lane_at]
        ks = [view(a[12], H, SLOT) for a in lane_at]
        ctxk = [view(a[13], KI, P) for a in lane_at]

        stats = [sb(f"stats{l}", [P, 6]) for l in range(NL)]
        mv = [sb(f"mv{l}", [P, 2]) for l in range(NL)]
        vare = [sb(f"vare{l}", [P, 1]) for l in range(NL)]
        rstd = [sb(f"rstd{l}", [P, 1]) for l in range(NL)]
        nmx = [sb(f"nmx{l}", [P, H]) for l in range(NL)]
        rsum = [sb(f"rsum{l}", [P, H]) for l in range(NL)]
        rinv = [sb(f"rinv{l}", [P, H]) for l in range(NL)]
        rm = [sb(f"rm{l}", [P, H, J]) for l in range(NL)]
        pp = [sb(f"pp{l}", [P, 2, H, 4]) for l in range(NL)]
        la = [sb(f"la{l}", [P, H, NLINE]) for l in range(NL)]
        lb = [sb(f"lb{l}", [P, H, NLINE]) for l in range(NL)]
        lsq = [sb(f"lsq{l}", [P, H]) for l in range(NL)]
        lrn = [sb(f"lrn{l}", [P, H]) for l in range(NL)]

        W0 = 12 * 2048
        a = put(W0, [512] * 4 + [1536, 512, 512])
        x0_wq, x0_wk, x0_wv, x0_wo = (view(a[i], KI, D) for i in range(4))
        a0_wqkv, a0_wg, a0_wout = view(a[4], KI, 3 * D), view(a[5], KI, D), view(a[6], KI, D)
        XN = a[6] + 512
        WT = XN + T * D
        wuT, wgT, wdT = view(WT, KI, F0), view(WT + 1536, KI, F0), view(WT + 3072, NF0, D)
        w_nat = [view(XN, 48, 32), view(XN + 1536, 48, 32), view(WT + 4608, 48, 32)]
        ug = view(0, 2 * NF0, NSEQ * L)
        xall = view(XN, T, D)
        xq = [view(W0 + i * 1024, TPB, D) for i in range(2)]
        xqT = [view(W0 + 2048 + i * 1024, KI, BLK) for i in range(2)]
        sg = [view(XN + i * 2048, 2048) for i in range(2)]
        oq = [view(W0 + i * 3072, NF0, BLK) for i in range(2)]
        f_stats = sb("f_stats", [P, T, 6])
        f_mv = sb("f_mv", [P, T, 2])
        f_ve = sb("f_ve", [P, T])
        f_rstd = sb("f_rstd", [P, T])
        wmax = sb("wmax", [P, 3, 48])
        wsc = sb("wsc", [P, 3, 48])
        winv = sb("winv", [P, 3, 48])
        amax = sb("amax", [P, 2 * NF0, NB, 1])
        pmax = sb("pmax", [P, 5])
        allmax = sb("allmax", [P, 5])
        qsc = sb("qsc", [P, 5])
        qinv = sb("qinv", [P, 5])
        QX, QU, QG, QS, QO = range(5)

        a = put(512, [KI * NSEQ * L, 1024, 2 * KI * S, 2 * KI * S])
        assert a[-1] + 2 * KI * S <= LANE
        qT_all = view(a[0], KI, NSEQ * L)
        c_qbd = [view(a[1] + i * 512, KI, 8, L) for i in range(2)]
        c_ctx = [view(a[2] + i * KI * S, KI, S) for i in range(2)]
        c_kT = [view(a[3] + i * KI * S, KI, S) for i in range(2)]
        a = put(LANE + 512, [1024, 512, G * S, 1024, 256, 256, 128, 128, 1024, 128])
        assert a[-1] + 128 <= R1
        c_v = [view(a[0] + i * 512, 2, D) for i in range(2)]
        c_vl = [view(a[1] + i * 256, D) for i in range(2)]
        c_p = view(a[2], G, S)
        c_pT = view(a[3], 4, 2, P)
        c_om = view(a[4], G, J * HD)
        c_oT = view(a[5], KI, P)
        c_last = view(a[6], KI, NSEQ)
        c_klast = view(a[7], KI, NSEQ)
        klast_seq = c_klast.rearrange("p a (n c) -> p a n c", c=1)
        c_vlm = view(a[8], G, D)
        c_plT = view(a[9], P)
        c_nmx = [sb(f"c_nmx{i}", [P, G]) for i in range(2)]
        c_sum = [sb(f"c_sum{i}", [P, G]) for i in range(2)]
        c_inv = sb("c_inv", [P, G])
        c_rm = sb("c_rm", [P, G, J])
        gmask = sb("gmask", [P, G, G])
        vl_dram = nc.dram_tensor("vl_dram", [NSEQ, G, D], F32, kind="Internal").ap()

        a = put(R1, [KI * F1, KI * F1, NF1 * F1, NF1 * F1, NF1 * D])
        f_w1, f_w2 = view(a[0], KI, F1), view(a[1], KI, F1)
        f_h1, f_h2 = view(a[2], NF1, F1), view(a[3], NF1, F1)
        f_w3 = view(a[4], NF1, D)
        a = put(0, [1024, 1024, 4096, 4096, 1024, 512])
        f_xn, f_xnT = view(a[0], TPB, D), view(a[1], KI, BLK)
        f_ha, f_hb = view(a[2], NF1, BLK), view(a[3], NF1, BLK)
        f_silu = view(a[4], 2, BLK)
        f_y = view(a[5], 2, D)
        g_stats = sb("g_stats", [P, TPB, 6])
        g_mv = sb("g_mv", [P, TPB, 2])
        g_ve = sb("g_ve", [P, TPB])
        g_rstd = sb("g_rstd", [P, TPB])

        magic = sb("magic", [P, 1])

        ps = ctx.enter_context(nc.psum_tensor("ps", [P, 8, 512], F32))

        in_const = sem("in_const")
        in_x = sem("in_x")
        in_w = {k: sem(f"in_w_{k}") for k in ("x0", "a0", "nat", "x1", "a1", "ffn")}
        posmask_ready, gate_bias_ready, pl_scale_ready, consts_made = map(
            sem, ("posmask_ready", "gate_bias_ready", "pl_scale_ready", "consts_made"))
        ctxk_in = lanes("ctxk_in")
        names = ("stats_ready mv_ready vare_ready rstd_ready xn_ready xnT_ready xnT_copied x_biased "
                 "qk_ready v_ready q_masked k_copied v_spread scores_ready scores_masked max_ready scores_shifted "
                 "probs_ready sum_ready pT_ready pT_copied o_ready o_normed oT_ready oT_copied "
                 "gate_ready gate_exp gate_plus gate_done y_ready x_updated "
                 "lines_in lines_step lines_sq lines_sum q_slots k_slots "
                 "qk_slots_ready q_evac q_copied").split()
        s = {n: sem(n) for n in names}


        def tile(n, l):
            return NL * n + l + 1

        dve_link = sem("dve_link")
        passed = {e: sem(f"{e}_passed") for e in ("act", "dve", "pool")}

        def stand(eng, e):
            eng.sem_inc(passed[e], 1)
        links = {}

        def link(eng, chain, ins):
            links[chain] = links.get(chain, 0) + 1
            ins.then_inc(chain, 1)
            eng.wait_ge(chain, links[chain])

        wT_quant, wT_turned, wT_copied = sem("wT_quant"), sem("wT_turned"), sem("wT_copied")
        f0_stats, f0_mv, f0_ve, f0_rstd, f0_pmax, f0_allmax, f0_scale = map(
            sem, ("f0_stats", "f0_mv", "f0_ve", "f0_rstd", "f0_pmax", "f0_allmax", "f0_scale"))
        f0_xq, f0_xT, f0_xTc, f0_ug, f0_ugc, f0_ugm = map(
            sem, ("f0_xq", "f0_xT", "f0_xTc", "f0_ug", "f0_ugc", "f0_ugm"))
        f0_gr, f0_gq, f0_sg, f0_sr, f0_g2, f0_g2r, f0_ur, f0_g3, f0_uq, f0_o = map(
            sem, ("f0_gr", "f0_gq", "f0_sg", "f0_sr", "f0_g2", "f0_g2r", "f0_ur", "f0_g3", "f0_uq", "f0_o"))
        f0_or, f0_oq, f0_y, f0_x = map(sem, ("f0_or", "f0_oq", "f0_y", "f0_x"))

        c_last_in, c_kl_ps, c_kl_done, c_vl_ps, c_vl_done, c_vl_out = map(
            sem, ("c_last_in", "c_kl_ps", "c_kl_done", "c_vl_ps", "c_vl_done", "c_vl_out"))
        q_all = sem("q_all")
        ctx_in = [sem(f"ctx_in{i}") for i in range(2)]
        vl_in = [sem(f"vl_in{i}") for i in range(2)]
        (k_ready, k_copied, klast_copied, v_ready, v_copied, c_q, c_s, c_max, c_exp, c_pt, c_ptc, c_pl, c_plc,
         c_o, c_rinv, c_rmd, c_omd, c_ot, c_otc, c_y, c_x) = map(sem, (
             "c_k_ready", "c_k_copied", "c_klast_copied", "c_v_ready", "c_v_copied", "c_q", "c_s", "c_max", "c_exp",
             "c_pt", "c_ptc", "c_pl", "c_plc", "c_o", "c_rinv", "c_rmd", "c_omd", "c_ot", "c_otc", "c_y", "c_x"))
        (g_st, g_mvd, g_ved, g_rs, g_xn, g_xT, g_xTc, g_ab, g_sil, g_h, g_h1, g_ge1, g_h2, g_ge2, g_w3, g_ys,
         g_x, g_out) = map(sem, ("g_st", "g_mvd", "g_ved", "g_rs", "g_xn", "g_xT", "g_xTc", "g_ab", "g_sil",
                                 "g_h", "g_h1", "g_ge1", "g_h2", "g_ge2", "g_w3", "g_ys", "g_x", "g_out"))

        free = {"act": (f0_xTc, f0_ugc, g_ge2), "dve": (f0_x, f0_g2, q_all, c_otc, c_rinv, g_ys),
                "pe": (f0_ug, f0_y, f0_xT, c_o, c_ot, c_y, g_xT)}

        RING1, RING2, RING3 = (4, 5, 0, 1), (2, 3, 4, 5), (0, 1)

        block = ctx.enter_context(nc.Block())

        X0, A0, A1 = "x0", "a0", "a1"
        BASE = {X0: 0, A0: NT, A1: 2 * NT}
        NORM = {X0: 0, A0: NT, A1: 3 * NT}
        WOUT = {X0: x0_wo, A0: a0_wout, A1: a1_wout}
        BOUT = {X0: BO0, A0: BOA, A1: BOB}
        BIAS_Q = {X0: BQ0, A0: BQA}
        BIAS_K = {X0: BK0, A0: BKA}
        BIAS_V = {X0: colb[:, BV0, :], A0: colb[:, BVA, :], A1: a1_bv[:, :]}
        N_CONST = 14
        xl = x[:, :, :].rearrange("p (i l) d -> p i l d", l=NL)
        bank = [[ps[:, 4 * l + i, :] for i in range(4)] for l in range(NL)]

        def halves(ap):
            return ap.rearrange("p (a b) -> p a b", b=P)

        @block.sync
        def _(sp):
            sp.dma_start(x[:, 0:2, :], A["x"][:, 0:2, :]).then_inc(in_x, 16)
            for d, n in ((ident, "ident"), (sel, "sel"), (mask8, "mask8"), (mask4, "mask4"), (causal, "causal"),
                         (colb, "colb"), (rowb, "rowb"), (posmask, "posbias"), (a1_bv, "a1_bv"),
                         (a1_bqk, "a1_bqk"), (plscale, "plscale"), (plsign, "plsign"), (gmask, "gmask"),
                         (w3s, "w3s")):
                sp.dma_start(d[:], A[n]).then_inc(in_const, 16)
            for d, n in ((x0_wq, "x0_wq"), (x0_wk, "x0_wk"), (x0_wv, "x0_wv"), (x0_wo, "x0_wo")):
                sp.dma_start(d, A[n]).then_inc(in_w["x0"], 16)

            def load_ctxk(l, i):
                sp.dma_start(ctxk[l], A["ctxk"][:, NL * i + l]).then_inc(ctxk_in[l], 16)

            for l in range(NL):
                load_ctxk(l, 0)
            sp.dma_start(x[:, 2:T, :], A["x"][:, 2:T, :]).then_inc(in_x, 16)
            for d, n in ((a0_wqkv, "a0_wqkv"), (a0_wg, "a0_wg"), (a0_wout, "a0_wout")):
                sp.dma_start(d, A[n]).then_inc(in_w["a0"], 16)
            for d, n in zip(w_nat, ("w_up", "w_gate", "w_down")):
                sp.dma_start(d, A[n]).then_inc(in_w["nat"], 16)
            for d, n in ((x1_wq, "x1_wq"), (x1_wk, "x1_wk"), (x1_wv, "x1_wv"), (x1_wo, "x1_wo")):
                sp.dma_start(d[:], A[n]).then_inc(in_w["x1"], 16)
            for d, n in ((a1_wqkv, "a1_wqkv"), (a1_wpl, "a1_wpl"), (a1_wout, "a1_wout"), (ffn_s, "ffn_s")):
                sp.dma_start(d[:], A[n]).then_inc(in_w["a1"], 16)
            with sp.Fori(1, NT) as i:
                for l in range(NL):
                    sp.wait_ge(s["v_ready"], tile(i - 1, l))
                    load_ctxk(l, i)

            sp.wait_ge(f0_x, 1 + T)
            sp.dma_start(c_last, A["ctx_last"]).then_inc(c_last_in, 16)
            for n in range(2):
                sp.dma_start(c_ctx[n], A["ctxT"][n]).then_inc(ctx_in[n], 16)
            for d, n in ((f_w1, "f_w1"), (f_w2, "f_w2"), (f_h1, "f_h1"), (f_h2, "f_h2"), (f_w3, "f_w3")):
                sp.dma_start(d, A[n]).then_inc(in_w["ffn"], 16)
            sp.wait_ge(c_vl_done, 1)
            sp.dma_start(vl_dram, c_vlm[0:NSEQ, :, :]).then_inc(c_vl_out, 16)
            sp.wait_ge(c_vl_out, 16)
            sp.dma_start(c_vl[0][0:G, :], vl_dram[0]).then_inc(vl_in[0], 16)

            def c_loads(i, last):
                for u in range(SPT):
                    n = SPT * i + u
                    if not (last and u == SPT - 1):
                        if not (isinstance(i, int) and n == 0):
                            sp.wait_ge(c_o, 1 + n)
                        sp.dma_start(c_vl[(u + 1) % 2][0:G, :], vl_dram[n + 1]).then_inc(vl_in[(u + 1) % 2], 16)
                    if not (last and u >= 2):
                        sp.wait_ge(v_ready, n + 1)
                        sp.dma_start(c_ctx[u % 2], A["ctxT"][n + 2]).then_inc(ctx_in[u % 2], 16)

            with sp.Fori(0, T - 1) as i:
                c_loads(i, False)
            c_loads(T - 1, True)
            for b in range(NB):
                sp.wait_ge(g_x, TPB * (b + 1))
                sp.dma_start(out[:, TPB * b:TPB * (b + 1), :], x[:, TPB * b:TPB * (b + 1), :]).then_inc(g_out, 16)
            sp.wait_ge(g_out, 16 * NB)

        @block.tensor
        def _(pe):
            for m in free["pe"]:
                pe.sem_inc(m, 1)
            mm = nc.tensor.matmul
            tr = nc.tensor.transpose

            def project(dst, w, src, fo):
                for ki in range(KI):
                    r = mm(dst, w[:, ki, fo * P:(fo + 1) * P], src[:, ki, :], start=(ki == 0), stop=(ki == KI - 1))
                return r

            def project_rows(dst, src, w):
                for ki in range(KI):
                    r = mm(dst, src[:, ki, :], w[:, ki], start=(ki == 0), stop=(ki == KI - 1))
                return r

            def p_turn(kind, l, n):
                pe.wait_ge(s["xn_ready"], tile(n, l))
                for ki in range(KI):
                    r = tr(halves(bank[l][0])[:, ki, :], xn[l][:, ki * P:(ki + 1) * P], ident[:])
                r.then_inc(s["xnT_ready"], 1)

            def p_project(kind, l, n):
                pe.wait_ge(s["xnT_copied"], tile(n - BASE[kind] + NORM[kind], l))
                qk = bank[l][1].rearrange("p (a b) -> p a b", b=P)
                if kind == A1:
                    project_rows(bank[l][1], xnT[l], a1_wqkv[:, :, 0:2 * D]).then_inc(s["qk_ready"], 1)
                    project_rows(bank[l][2][:, D:D + 8 * H], xnT[l],
                                 a1_wpl[:, :, :, :].rearrange("p k a b -> p k (a b)"))
                    project_rows(bank[l][2][:, 0:D], xnT[l], a1_wqkv[:, :, 2 * D:3 * D]).then_inc(s["v_ready"], 1)
                    return
                wq = x0_wq if kind == X0 else a0_wqkv[:, :, 0:D]
                wk = x0_wk if kind == X0 else a0_wqkv[:, :, D:2 * D]
                wv = x0_wv if kind == X0 else a0_wqkv[:, :, 2 * D:3 * D]
                src = ctxk[l] if kind == X0 else xnT[l]
                for fo in range(KI):
                    project(qk[:, fo, :], wq, xnT[l], fo)
                if kind == X0:
                    pe.wait_ge(ctxk_in[l], 16 * (n + 1))
                for fo in range(KI):
                    r = project(qk[:, KI + fo, :], wk, src, fo)
                r.then_inc(s["qk_ready"], 1)
                project_rows(bank[l][2][:, 0:D], src, wv).then_inc(s["v_ready"], 1)
                if kind == A0:
                    for fo in range(KI):
                        r = project(halves(bank[l][0])[:, fo, :], a0_wg, xnT[l], fo)
                    r.then_inc(s["gate_ready"], 1)

            def p_slots(kind, l, n):
                pe.wait_ge(s["q_slots"], tile(n - BASE[A1], l))
                for g in range(G):
                    r = tr(bank[l][1][:, g * P:(g + 1) * P], qs[l][:, J * g:J * (g + 1), :], ident[:])
                pe.wait_ge(s["k_slots"], tile(n - BASE[A1], l))
                for g in range(G):
                    r = tr(bank[l][3][:, g * P:(g + 1) * P], ks[l][:, J * g:J * (g + 1), :], ident[:])
                r.then_inc(s["qk_slots_ready"], 1)

            def p_scores(kind, l, n):
                pe.wait_ge(s["q_masked"], tile(n, l))
                pe.wait_ge(s["k_copied"], tile(n, l))
                for g in range(G):
                    for b in range(SPT):
                        if kind == A1:
                            q = qbd[l][:, (g * SPT + b) * P:(g * SPT + b + 1) * P]
                            k = kT[l][:, g * P + b * L:g * P + (b + 1) * L]
                        else:
                            at = (((g // 2) * SPT + b) * 2 + g % 2) * P
                            q = qbd[l][:, at:at + P]
                            k = kT[l][:, (g // 2) * P + b * L:(g // 2) * P + (b + 1) * L]
                        r = mm(bank[l][3][:, g * P + b * L:g * P + (b + 1) * L], q, k, start=True, stop=True)
                r.then_inc(s["scores_ready"], 1)

            def p_turn_probs(kind, l, n):
                pe.wait_ge(s["probs_ready"], tile(n, l))
                for g in range(G):
                    r = tr(bank[l][1][:, g * P:(g + 1) * P], pr[l][:, g, :], ident[:])
                r.then_inc(s["pT_ready"], 1)

            def p_values(kind, l, n):
                pe.wait_ge(s["v_spread"], tile(n, l))
                pe.wait_ge(s["pT_copied"], tile(n, l))
                for g in range(G):
                    o = bank[l][2 + g // 2].rearrange("p (b g e) -> p b g e", g=2, e=J * HD)[:, :, g % 2, :]
                    r = mm(o, pT[l][:, g, :], vbd[l][:, :, g * J * HD:(g + 1) * J * HD], start=True, stop=True)
                r.then_inc(s["o_ready"], 1)

            def p_gather(kind, l, n):
                if kind == A0:
                    pe.wait_ge(s["gate_exp"], tile(n - BASE[A0], l))
                pe.wait_ge(s["o_normed"], tile(n, l))
                for half in range(KI):
                    for b in range(SPT):
                        r = mm(bank[l][0][:, D + half * P + b * L:D + half * P + (b + 1) * L],
                               om[l][:, (half * SPT + b) * P:(half * SPT + b + 1) * P], sel[:], start=True, stop=True)
                r.then_inc(s["oT_ready"], 1)

            def p_out(kind, l, n):
                pe.wait_ge(s["oT_copied"], tile(n, l))
                project_rows(bank[l][2][:, 0:D], oT[l], WOUT[kind]).then_inc(s["y_ready"], 1)

            pe.wait_ge(in_const, 16 * N_CONST)

            def attention(kind, steps, w):
                pe.wait_ge(in_w[w], 16 * {"x0": 4, "a0": 3, "a1": 4}[w])
                with pe.Fori(0, NT) as i:
                    for step in steps:
                        for l in range(NL):
                            step(kind, l, i + (NORM if step is p_turn else BASE)[kind])

            steps = [p_turn, p_project, p_scores, p_turn_probs, p_values, p_gather, p_out]
            attention(X0, steps, "x0")
            attention(A0, steps, "a0")

            for l in range(NL):
                pe.wait_ge(s["x_updated"], tile(2 * NT - 1, l))
            k = 0
            for m in range(3):
                pe.wait_ge(wT_quant, m + 1)
                w = w_nat[m].rearrange("p a b -> p (a b)")
                a_n, b_n = (NF0, KI) if m < 2 else (KI, NF0)
                for bi in range(b_n):
                    for ai in range(a_n):
                        at = (bi * a_n + ai) * P
                        if k % 4 == 0 and k // 4 >= 8:
                            pe.wait_ge(wT_copied, k // 4 - 7)
                        r = tr(ps[:, (k // 4) % 8, (k % 4) * P:(k % 4 + 1) * P],
                               w[:, (ai * b_n + bi) * P:(ai * b_n + bi + 1) * P], ident[:])
                        k += 1
                        if k % 4 == 0:
                            r.then_inc(wT_turned, 1)
            pe.wait_ge(wT_copied, 9)

            with pe.Fori(0, NB // 2) as i:
                for u in range(2):
                    b = 2 * i + u
                    pe.wait_ge(f0_xq, b + 1)
                    pe.wait_ge(f0_xTc, 1 + 2 * b)
                    for ki in range(KI):
                        for t in range(TPB):
                            r = tr(ps[:, 6 + ki, t * P:(t + 1) * P], xq[u][:, t, ki * P:(ki + 1) * P], ident[:])
                        r.then_inc(f0_xT, 1)
                    pe.wait_ge(f0_xTc, 1 + 2 * b + 2)
                    for f in range(2 * NF0):
                        w = wuT if f < NF0 else wgT
                        fb = ps[:, f % 4, :]
                        if f >= 4:
                            pe.wait_ge(f0_ugc, 1 + 2 * NF0 * b + f - 3)
                        else:
                            pe.wait_ge(f0_ugc, 1 + 2 * NF0 * b)
                        project(fb, w, xqT[u], f % NF0).then_inc(f0_ug, 1)
            with pe.Fori(0, NB // 2) as i:
                for u in range(2):
                    b = 2 * i + u
                    pe.wait_ge(f0_oq, NF0 * (b + 1))
                    pe.wait_ge(f0_x, 1 + TPB * 2 * i)
                    for t in range(TPB):
                        for f in range(NF0):
                            r = mm(ps[:, 4 * u + t, 0:D], oq[u][:, f, t * P:(t + 1) * P], wdT[:, f, :],
                                   start=(f == 0), stop=(f == NF0 - 1))
                        r.then_inc(f0_y, 1)

            pe.wait_ge(f0_x, 1 + T)
            pe.wait_ge(in_w["x1"], 64)
            pe.wait_ge(c_last_in, 16)
            for fo in range(KI):
                r = project(ps[:, 2, fo * NSEQ:(fo + 1) * NSEQ], x1_wk, c_last, fo)
            r.then_inc(c_kl_ps, 1)
            project_rows(ps[0:NSEQ, 3, 0:D], c_last, x1_wv).then_inc(c_vl_ps, 1)
            with pe.Fori(0, NT) as i:
                for l in range(NL):
                    p_turn(None, l, i + 2 * NT)
                for l in range(NL):
                    pe.wait_ge(s["xnT_copied"], tile(i + 2 * NT, l))
                    pe.wait_ge(q_all, 1 + NL * i)
                    for fo in range(KI):
                        r = project(bank[l][1][:, fo * P:(fo + 1) * P], x1_wq, xnT[l], fo)
                    r.then_inc(s["q_evac"], 1)

            kb, vb, tb, ob = (ps[:, i, :] for i in (4, 5, 6, 7))
            o_all = ob[:, 0:D].rearrange("p (g e) -> p g e", g=G)

            def c_keys(par):
                for fo in range(KI):
                    for ki in range(KI):
                        r = mm(kb[:, fo * D:(fo + 1) * D], x1_wk[:, ki, fo * P:(fo + 1) * P],
                               c_ctx[par][:, ki, 0:2 * P], start=(ki == 0), stop=(ki == KI - 1))
                r.then_inc(k_ready, 1)

            def c_values(par):
                for c in range(2):
                    for ki in range(KI):
                        r = mm(vb[:, c * D:(c + 1) * D], c_ctx[par][:, ki, c * P:(c + 1) * P], x1_wv[:, ki, :],
                               start=(ki == 0), stop=(ki == KI - 1))
                r.then_inc(v_ready, 1)

            def c_scores(par):
                for g in range(G):
                    mm(ps[:, g, 0:S], c_qbd[par][:, g // 2, J * (g % 2):J * (g % 2 + 1), :], c_kT[par][:, g // 2, :],
                       start=True, stop=True).then_inc(c_s, 1)

            def c_step(i, u, last):
                n = SPT * i + u
                par = u % 2
                pe.wait_ge(c_exp, 4 * n + 4)
                for g in range(G):
                    if g == 2:
                        if not (last and u == SPT - 1):
                            pe.wait_ge(k_copied, n + 2)
                    dst = tb if g < 2 else kb
                    for c in range(2):
                        at = ((g % 2) * 2 + c) * P
                        r = tr(dst[:, at:at + P], c_p[:, g, c * P:(c + 1) * P], ident[:])
                    if g % 2:
                        r.then_inc(c_pt, 1)
                pe.wait_ge(c_otc, 1 + n)
                tr(ob[0:G, 320:320 + P], c_p[:, :, 2 * P], ident[:]).then_inc(c_pl, 1)
                if not (last and u == SPT - 1):
                    pe.wait_ge(klast_copied, n + 2)
                    pe.wait_ge(c_q, n + 2)
                    c_scores((u + 1) % 2)
                pe.wait_ge(c_plc, n + 1)
                pe.wait_ge(v_copied, n + 1)
                for g in range(G):
                    if g % 2 == 0:
                        pe.wait_ge(c_ptc, 2 * n + 1 + g // 2)
                    for c in range(2):
                        mm(o_all[:, g, :], c_pT[:, g, c, :], c_v[par][:, c, g * J * HD:(g + 1) * J * HD],
                           start=(g == 0 and c == 0), stop=False, skip_group_check=True)
                pe.wait_ge(vl_in[par], 16 * (SPT // 2 * i + u // 2 + 1))
                mm(ob[:, 0:D], c_plT[0:G, :], c_vl[par][0:G, :], start=False, stop=True,
                   skip_group_check=True).then_inc(c_o, 1)
                more = not (last and u >= 2)
                if more:
                    pe.wait_ge(ctx_in[par], 16 * (SPT // 2 * i + (u + 2) // 2 + 1))
                    c_keys(par)
                pe.wait_ge(c_omd, n + 1)
                pe.wait_ge(c_otc, 1 + n)
                for half in range(KI):
                    r = mm(ob[:, D + half * L:D + (half + 1) * L], c_om[:, 2 * half:2 * half + 2, :], sel[:],
                           start=True, stop=True)
                r.then_inc(c_ot, 1)
                if not (last and u == SPT - 1):
                    pe.wait_ge(v_copied, n + 2)
                if u == SPT - 1:
                    pe.wait_ge(c_otc, 1 + n + 1)
                    project_rows(vb[:, 0:D], c_oT, x1_wo).then_inc(c_y, 1)
                if more:
                    if u == SPT - 1:
                        pe.wait_ge(c_x, i + 1)
                    c_values(par)

            for l in range(NL):
                pe.wait_ge(q_all, 1 + tile(NT - 1, l))
            pe.wait_ge(c_kl_done, 1)
            pe.wait_ge(c_vl_done, 1)
            pe.wait_ge(ctx_in[0], 16)
            c_keys(0)
            c_values(0)
            pe.wait_ge(k_copied, 1)
            pe.wait_ge(klast_copied, 1)
            pe.wait_ge(c_q, 1)
            c_scores(0)
            pe.wait_ge(ctx_in[1], 16)
            c_keys(1)
            pe.wait_ge(v_copied, 1)
            c_values(1)
            with pe.Fori(0, T - 1) as i:
                for u in range(SPT):
                    c_step(i, u, False)
            for u in range(SPT):
                c_step(T - 1, u, True)

            pe.wait_ge(c_x, T)
            attention(A1, [p_turn, p_project, p_slots, p_scores, p_turn_probs, p_values, p_gather, p_out], "a1")

            for l in range(NL):
                pe.wait_ge(s["x_updated"], tile(3 * NT - 1, l))
            pe.wait_ge(in_w["ffn"], 16 * 5)

            def g_turn(b):
                pe.wait_ge(g_xn, b + 1)
                for ki in range(KI):
                    for t in range(TPB):
                        r = tr(ps[:, 6 + ki, t * P:(t + 1) * P], f_xn[:, t, ki * P:(ki + 1) * P], ident[:])
                    r.then_inc(g_xT, 1)

            def g_block(b, last):
                pe.wait_ge(g_xTc, 2 * b + 2)
                for o in range(NF1):
                    if o >= 2:
                        pe.wait_ge(g_h, NF1 * b + o - 1)
                    else:
                        pe.wait_ge(g_ge2, 1 + NF1 * b)
                        pe.wait_ge(g_ys, 1 + TPB * b)
                    project(ps[:, o % 2, :], f_w1, f_xnT, o)
                    project(ps[:, 2 + o % 2, :], f_w2, f_xnT, o).then_inc(g_ab, 1)
                for h, (w, src, done, prev, read, ring) in enumerate((
                        (f_h1, f_ha, g_h1, g_h, g_ge1, RING1), (f_h2, f_hb, g_h2, g_ge1, g_ge2, RING2))):
                    for o in range(NF1):
                        if o >= 4:
                            pe.wait_ge(read, h + NF1 * b + o - 3)
                        for k in range(NF1):
                            if o == 0:
                                pe.wait_ge(prev, NF1 * b + k + 1)
                            r = mm(ps[:, ring[o % 4], :], w[:, k, o * P:(o + 1) * P], src[:, k, :],
                                   start=(k == 0), stop=(k == NF1 - 1))
                        r.then_inc(done, 1)
                    if h == 0 and not last:
                        g_turn(b + 1)
                for t in range(TPB):
                    if t >= 2:
                        pe.wait_ge(g_ys, 1 + TPB * b + t - 1)
                    else:
                        pe.wait_ge(g_ys, 1 + TPB * b)
                    for k in range(NF1):
                        if t == 0:
                            pe.wait_ge(g_ge2, 1 + NF1 * b + k + 1)
                        r = mm(ps[:, RING3[t % 2], 0:D], f_ha[:, k, t * P:(t + 1) * P], f_w3[:, k, :],
                               start=(k == 0), stop=(k == NF1 - 1))
                    r.then_inc(g_w3, 1)

            g_turn(0)
            with pe.Fori(0, NB - 1) as b:
                g_block(b, False)
            g_block(NB - 1, True)

        @block.scalar
        def _(act):
            for m in free["act"]:
                act.sem_inc(m, 1)
            af = nc.scalar.activation

            def a_xnT(kind, l, n):
                act.wait_ge(s["xnT_ready"], tile(n, l))
                af(xnT[l], halves(bank[l][0])[:, 0:KI, :], ACT.Copy).then_inc(s["xnT_copied"], 1)

            def a_keys(kind, l, n):
                if kind == A1:
                    act.wait_ge(s["qk_slots_ready"], tile(n - BASE[A1], l))
                    af(kT[l], bank[l][3], ACT.Copy).then_inc(s["k_copied"], 1)
                    return
                act.wait_ge(s["qk_ready"], tile(n, l))
                for fo in range(KI):
                    r = af(qT[l][:, fo * P:(fo + 1) * P], bank[l][1][:, fo * P:(fo + 1) * P],
                           ACT.Identity, bias=colb[:, BIAS_Q[kind], fo:fo + 1])
                r.then_inc(s["q_copied"], 1)
                for fo in range(KI):
                    r = af(kT[l][:, fo * P:(fo + 1) * P], bank[l][1][:, (KI + fo) * P:(KI + fo + 1) * P],
                           ACT.Identity, bias=colb[:, BIAS_K[kind], fo:fo + 1])
                r.then_inc(s["k_copied"], 1)

            def a_spread(kind, l, n):
                act.wait_ge(s["v_ready"], tile(n, l))
                for b in range(SPT):
                    rows = slice(b * L, (b + 1) * L)
                    r = af(vbd[l][rows, b, :], bank[l][2][rows, 0:D], ACT.Copy)
                r.then_inc(s["v_spread"], 1)

            def a_lines(kind, l, n):
                act.wait_ge(s["v_ready"], tile(n, l))
                af(pp[l][:, :, :, :], bank[l][2][:, D:D + 8 * H].rearrange("p (a h c) -> p a h c", a=2, c=4),
                   ACT.Copy).then_inc(s["lines_in"], 1)

            def a_gate(kind, l, n):
                act.wait_ge(s["gate_ready"], tile(n - BASE[A0], l))
                for fo in range(KI):
                    r = af(gT[l][:, fo, :], halves(bank[l][0])[:, fo, :], ACT.Exp, scale=-1.0,
                           bias=nbg[:, fo:fo + 1])
                r.then_inc(s["gate_exp"], 1)

            def a_exp(kind, l, n):
                act.wait_ge(s["scores_shifted"], tile(n, l))
                af(pr[l].rearrange("p g (b k) -> p (g b) k", k=L), sc[l], ACT.Exp).then_inc(s["probs_ready"], 1)

            def a_pT(kind, l, n):
                act.wait_ge(s["pT_ready"], tile(n, l))
                af(pT[l], bank[l][1].rearrange("p (g t) -> p g t", t=P), ACT.Copy).then_inc(s["pT_copied"], 1)

            act.wait_ge(in_const, 16 * N_CONST)
            act.wait_ge(gate_bias_ready, 1)
            act.wait_ge(consts_made, 1)

            def attention(kind, steps):
                with act.Fori(0, NT) as i:
                    for step in steps:
                        for l in range(NL):
                            step(kind, l, i + (NORM if step is a_xnT else BASE)[kind])

            attention(X0, [a_xnT, a_keys, a_spread, a_exp, a_pT])
            attention(A0, [a_xnT, a_keys, a_spread, a_gate, a_exp, a_pT])

            for m in range(3):
                for c in range(3):
                    act.wait_ge(wT_turned, 3 * m + c + 1)
                    at = WT + 1536 * m + 512 * c
                    af(view(at, 512), ps[:, (3 * m + c) % 8, :], ACT.Copy).then_inc(wT_copied, 1)
            ugb = ug.rearrange("p f (b t) -> p f b t", t=BLK)
            with act.Fori(0, NB // 2) as i:
                for u in range(2):
                    b = 2 * i + u
                    for ki in range(KI):
                        act.wait_ge(f0_xT, 1 + 2 * b + ki + 1)
                        act.wait_ge(f0_ug, 1 + 2 * NF0 * b)
                        af(xqT[u][:, ki, :], ps[:, 6 + ki, :], ACT.Copy).then_inc(f0_xTc, 1)
                    for f in range(2 * NF0):
                        act.wait_ge(f0_ug, 1 + 2 * NF0 * b + f + 1)
                        stand(act, "act")
                        af(ugb[:, f, b, :], ps[:, f % 4, :], ACT.Copy).then_inc(f0_ugc, 1)
            act.wait_ge(f0_scale, 2)
            with act.Fori(0, NF0 // 2) as i:
                for u in range(2):
                    f = 2 * i + u
                    af(ug[:, f + NF0, :], ug[:, f + NF0, :], ACT.Identity, scale=qinv[:, QG:QG + 1],
                       bias=magic[:, :]).then_inc(f0_gr, 1)
                for u in range(2):
                    f = 2 * i + u
                    act.wait_ge(f0_gq, f + 1)
                    act.wait_ge(f0_g2, 1 + 2 * i)
                    stand(act, "act")
                    af(sg[u], ug[:, f + NF0, :], ACT.Sigmoid).then_inc(f0_sg, 1)
            act.wait_ge(f0_scale, 3)
            with act.Fori(0, NF0) as f:
                af(ug[:, f + NF0, :], ug[:, f + NF0, :], ACT.Identity, scale=qinv[:, QS:QS + 1],
                   bias=magic[:, :]).then_inc(f0_g2r, 1)
                af(ug[:, f, :], ug[:, f, :], ACT.Identity, scale=qinv[:, QU:QU + 1],
                   bias=magic[:, :]).then_inc(f0_ur, 1)
            act.wait_ge(f0_scale, 4)
            with act.Fori(0, NB // 2) as i:
                for u in range(2):
                    b = 2 * i + u
                    act.wait_ge(f0_y, 1 + TPB * 2 * i)
                    stand(act, "act")
                    for f in range(NF0):
                        af(oq[u][:, f, :], ugb[:, f, b, :], ACT.Identity, scale=qinv[:, QO:QO + 1],
                           bias=magic[:, :]).then_inc(f0_or, 1)

            act.wait_ge(c_kl_ps, 1)
            act.wait_ge(f0_x, 1 + T)
            for fo in range(KI):
                r = af(c_klast[:, fo, :], ps[:, 2, fo * NSEQ:(fo + 1) * NSEQ], ACT.Identity,
                       bias=colb[:, BK1, fo:fo + 1])
            r.then_inc(c_kl_done, 1)
            with act.Fori(0, NT) as i:
                for l in range(NL):
                    a_xnT(None, l, i + 2 * NT)

            def c_keys(par, count):
                act.wait_ge(k_ready, count)
                for fo in range(KI):
                    r = af(c_kT[par][:, fo, 0:2 * P], ps[:, 4, fo * D:(fo + 1) * D], ACT.Identity,
                           bias=colb[:, BK1, fo:fo + 1])
                r.then_inc(k_copied, 1)

            def c_values(par, count):
                act.wait_ge(v_ready, count)
                af(c_v[par].rearrange("p c e -> p (c e)"), ps[:, 5, :], ACT.Copy).then_inc(v_copied, 1)

            def c_exps(par, n):
                for g in range(G):
                    act.wait_ge(c_max, G * n + g + 1)
                    af(c_p[:, g, :], ps[:, g, 0:S], ACT.Exp, bias=c_nmx[par][:, g:g + 1],
                       accum_out=c_sum[par][:, g:g + 1]).then_inc(c_exp, 1)

            def c_step(i, u, last):
                n = SPT * i + u
                act.wait_ge(c_pl, n + 1)
                act.wait_ge(c_o, 1 + n)
                af(c_plT[0:G, :], ps[0:G, 7, 320:320 + P], ACT.Copy).then_inc(c_plc, 1)
                if not (last and u == SPT - 1):
                    act.wait_ge(c_rinv, 1 + n)
                    c_exps((u + 1) % 2, n + 1)
                if not (last and u >= 2):
                    c_keys(u % 2, n + 3)
                    c_values(u % 2, n + 3)

            for l in range(NL):
                act.wait_ge(q_all, 1 + tile(NT - 1, l))
            c_keys(0, 1)
            c_values(0, 1)
            c_exps(0, 0)
            c_keys(1, 2)
            c_values(1, 2)
            with act.Fori(0, T - 1) as i:
                for u in range(SPT):
                    c_step(i, u, False)
            for u in range(SPT):
                c_step(T - 1, u, True)
            act.wait_ge(c_x, T)
            act.wait_ge(consts_made, 2)
            attention(A1, [a_xnT, a_lines, a_spread, a_keys, a_exp, a_pT])

            for l in range(NL):
                act.wait_ge(s["x_updated"], tile(3 * NT - 1, l))

            def g_turned(b):
                for ki in range(KI):
                    act.wait_ge(g_xT, 1 + 2 * b + ki + 1)
                    af(f_xnT[:, ki, :], ps[:, 6 + ki, :], ACT.Copy).then_inc(g_xTc, 1)

            def g_block(b, last):
                for o in range(NF1):
                    act.wait_ge(g_ab, NF1 * b + o + 1)
                    if o >= 2:
                        act.wait_ge(g_h, NF1 * b + o - 1)
                    af(f_silu[:, o % 2, :], ps[:, o % 2, :], ACT.Silu, scale=ffn_s[:, 0, o:o + 1]).then_inc(g_sil, 1)
                for o in range(NF1):
                    act.wait_ge(g_h1, NF1 * b + o + 1)
                    af(f_hb[:, o, :], ps[:, RING1[o % 4], :], ACT.Gelu, scale=ffn_s[:, 2, o:o + 1]).then_inc(g_ge1, 1)
                if not last:
                    g_turned(b + 1)
                for o in range(NF1):
                    act.wait_ge(g_h2, NF1 * b + o + 1)
                    af(f_ha[:, o, :], ps[:, RING2[o % 4], :], ACT.Gelu, scale=ffn_s[:, 3, o:o + 1]).then_inc(g_ge2, 1)

            g_turned(0)
            with act.Fori(0, NB - 1) as b:
                g_block(b, False)
            g_block(NB - 1, True)

        @block.vector
        def _(dve):
            for m in free["dve"]:
                dve.sem_inc(m, 1)
            v = nc.vector

            def d_norm(kind, l, i, n):
                v.bn_stats(stats[l][:, :], xl[:, i, l, :]).then_inc(s["stats_ready"], 1)
                dve.wait_ge(s["stats_ready"], tile(n, l))
                stand(dve, "dve")
                v.bn_aggr(mv[l][:, :], stats[l][:, :]).then_inc(s["mv_ready"], 1)

            def d_scale(kind, l, i, n):
                dve.wait_ge(s["rstd_ready"], tile(n, l))
                v.tensor_scalar(xn[l], xl[:, i, l, :], mv[l][:, 0:1], rstd[l][:, :], ALU.subtract, ALU.mult)\
                    .then_inc(s["xn_ready"], 1)

            def d_queries(kind, l, i, n):
                if kind == A1:
                    dve.wait_ge(s["qk_slots_ready"], tile(n - BASE[A1], l))
                    q = bank[l][1].rearrange("p (c q) -> p c q", q=L).unsqueeze(2).broadcast_to([P, H, J, L])
                    m = mask4[:, :].unsqueeze(1).unsqueeze(3).broadcast_to([P, H, J, L])
                    v.tensor_tensor(qbd[l].rearrange("p (c j q) -> p c j q", j=J, q=L), q, m, ALU.mult)\
                        .then_inc(s["q_masked"], 1)
                    return
                dve.wait_ge(s["q_copied"], tile(n, l))
                q = qT[l].rearrange("p (c q) -> p c q", q=L).unsqueeze(2).broadcast_to([P, 8, 8, L])
                m = mask8[:, :].unsqueeze(1).unsqueeze(3).broadcast_to([P, 8, 8, L])
                v.tensor_tensor(qbd[l].rearrange("p (c h q) -> p c h q", h=8, q=L), q, m, ALU.mult)\
                    .then_inc(s["q_masked"], 1)

            def d_slots(kind, l, i, n):
                m = n - BASE[A1]
                dve.wait_ge(s["qk_ready"], tile(n, l))
                for d, c, done in ((qs[l], 0, "q_evac"), (ks[l], 1, "k_slots")):
                    src = bank[l][1][:, c * D:(c + 1) * D].rearrange("p (h e) -> p h e", e=HD)
                    b = a1_bqk[:, c * D:(c + 1) * D].rearrange("p (h e) -> p h e", e=HD)
                    r = v.tensor_tensor(d[:, :, 0:HD], src, b, ALU.add)
                    if c == 1:
                        r.then_inc(s["q_evac"], 1)
                dve.wait_ge(s["lines_sq"], tile(m, l))
                v.tensor_reduce(lsq[l][:, :], lb[l][:, :, :], AX.X, ALU.add).then_inc(s["lines_sum"], 1)
                dve.wait_ge(s["lines_sum"], 2 * (NL * m + l) + 1)
                v.tensor_scalar(lsq[l][:, :], lsq[l][:, :], 1e-24, None, ALU.max).then_inc(s["lines_sum"], 1)

            def d_mask(kind, l, i, n):
                dve.wait_ge(s["scores_ready"], tile(n, l))
                mk = posmask if kind == A0 else causal
                v.scalar_tensor_tensor(sc[l].rearrange("p c k -> p (c k)"), bank[l][3], 0.25, mk[:, :],
                                       ALU.mult, ALU.add).then_inc(s["scores_masked"], 1)

            def d_max(kind, l, i, n):
                dve.wait_ge(s["scores_masked"], tile(n, l))
                v.tensor_reduce(nmx[l][:, :], sc[l], AX.X, ALU.max, negate=True).then_inc(s["max_ready"], 1)

            def d_shift(kind, l, i, n):
                dve.wait_ge(s["max_ready"], tile(n, l))
                v.tensor_tensor(sc[l], sc[l], nmx[l][:, :].unsqueeze(2).broadcast_to([P, H, L]), ALU.add)\
                    .then_inc(s["scores_shifted"], 1)

            def d_sums(kind, l, i, n):
                dve.wait_ge(s["probs_ready"], tile(n, l))
                v.tensor_reduce(rsum[l][:, :], pr[l].rearrange("p g (b k) -> p (g b) k", k=L), AX.X, ALU.add)\
                    .then_inc(s["sum_ready"], 1)
                dve.wait_ge(s["sum_ready"], 3 * NL * n + 2 * l + 1)
                v.reciprocal(rinv[l][:, :].rearrange("p (a b g) -> p a g b", a=KI, g=2),
                             rsum[l][:, :].rearrange("p (a g b) -> p a g b", a=KI, g=2)).then_inc(s["sum_ready"], 1)

            def d_rm(kind, l, i, n):
                dve.wait_ge(s["sum_ready"], 3 * NL * n + 2 * l + 2)
                v.tensor_tensor(rm[l][:, :, :], rinv[l][:, :].unsqueeze(2).broadcast_to([P, H, J]),
                                mask4[:, :].unsqueeze(1).broadcast_to([P, H, J]), ALU.mult)\
                    .then_inc(s["sum_ready"], 1)

            def d_gate1(kind, l, i, n):
                m = n - BASE[A0]
                dve.wait_ge(s["gate_exp"], tile(m, l))
                v.tensor_scalar(gT[l], gT[l], 1.0, None, ALU.add).then_inc(s["gate_plus"], 1)

            def d_gate2(kind, l, i, n):
                m = n - BASE[A0]
                dve.wait_ge(s["gate_plus"], tile(m, l))
                v.reciprocal(gT[l], gT[l]).then_inc(s["gate_done"], 1)

            def d_own(kind, l, i, n):
                dve.wait_ge(s["sum_ready"], 3 * NL * n + 2 * NL + l + 1)
                dve.wait_ge(s["o_ready"], tile(n, l))
                o = ps[:, 4 * l + 2:4 * l + 4, :].rearrange("p k (c j e) -> p (k c) j e", j=J, e=HD)
                v.tensor_tensor(om[l].rearrange("p (c j e) -> p c j e", j=J, e=HD), o,
                                rm[l][:, :, :].unsqueeze(3).broadcast_to([P, H, J, HD]), ALU.mult)\
                    .then_inc(s["o_normed"], 1)

            def d_oT(kind, l, i, n):
                dve.wait_ge(s["oT_ready"], tile(n, l))
                src = bank[l][0][:, D:2 * D].rearrange("p (a t) -> p a t", t=P)
                if kind == A0:
                    dve.wait_ge(s["gate_done"], tile(n - BASE[A0], l))
                    for fo in range(KI):
                        r = v.scalar_tensor_tensor(oT[l][:, fo, :], src[:, fo, :], colb[:, BVA, fo:fo + 1],
                                                   gT[l][:, fo, :], ALU.add, ALU.mult)
                else:
                    r = v.tensor_tensor(oT[l], src, BIAS_V[kind].unsqueeze(2).broadcast_to([P, KI, P]), ALU.add)
                r.then_inc(s["oT_copied"], 1)

            def d_add(kind, l, i, n):
                dve.wait_ge(s["y_ready"], tile(n, l))
                dve.wait_ge(s["x_biased"], tile(n - BASE[kind] + NORM[kind], l))
                v.tensor_tensor(xl[:, i, l, :], xl[:, i, l, :], bank[l][2][:, 0:D], ALU.add)\
                    .then_inc(s["x_updated"], 1)

            def attention(kind, steps):
                with dve.Fori(0, NT) as i:
                    for step in steps:
                        for l in range(NL):
                            step(kind, l, i, i + (NORM if step in (d_norm, d_scale) else BASE)[kind])

            v.memset(magic[:, :], MAGIC)
            for l in range(NL):
                v.memset(vbd[l], 0.0)
            v.memset(minus_half[:, :], -0.5).then_inc(consts_made, 1)
            dve.wait_ge(in_const, 16 * N_CONST)
            v.tensor_scalar(nbg[:, :], colb[:, BG, :], -1.0, None, ALU.mult).then_inc(gate_bias_ready, 1)
            v.tensor_tensor(posmask[:, :], posmask[:, :], causal[:, :], ALU.add).then_inc(posmask_ready, 1)
            v.tensor_scalar(plscale[:, :], plscale[:, :], 4.0, None, ALU.mult).then_inc(pl_scale_ready, 1)
            dve.wait_ge(pl_scale_ready, 1)
            v.tensor_tensor(plsc[:, :, :], plscale[:, :].unsqueeze(2).broadcast_to([P, H, NLINE]),
                            plsign[:, :].unsqueeze(1).broadcast_to([P, H, NLINE]), ALU.mult)\
                .then_inc(pl_scale_ready, 1)
            dve.wait_ge(posmask_ready, 1)
            dve.wait_ge(in_x, 32)
            common = [d_mask, d_max, d_shift, d_sums, d_rm]
            attention(X0, [d_norm, d_scale, d_queries] + common + [d_own, d_oT, d_add])
            for l in range(NL):
                dve.wait_ge(s["x_updated"], tile(NT - 1, l))
            attention(A0, [d_norm, d_scale, d_queries] + common[:3] + [d_gate1, d_gate2] + common[3:]
                      + [d_own, d_oT, d_add])
            for l in range(NL):
                dve.wait_ge(s["x_updated"], tile(2 * NT - 1, l))

            dve.wait_ge(in_w["nat"], 48)
            for m in range(3):
                w = w_nat[m]
                link(dve, dve_link, v.tensor_reduce(wmax[:, m, :], w, AX.X, ALU.max, apply_absolute_value=True))
                link(dve, dve_link, v.tensor_scalar(wsc[:, m, :], wmax[:, m, :], 1.0 / 7.0, 1e-12, ALU.mult, ALU.max))
                link(dve, dve_link, v.reciprocal(winv[:, m, :], wsc[:, m, :]))
                link(dve, dve_link, v.tensor_tensor(w, w, winv[:, m, :].unsqueeze(2).broadcast_to([P, 48, 32]), ALU.mult))
                link(dve, dve_link, v.tensor_scalar(w, w, MAGIC, None, ALU.add))
                v.scalar_tensor_tensor(w, w, -MAGIC, wsc[:, m, :].unsqueeze(2).broadcast_to([P, 48, 32]),
                                       ALU.add, ALU.mult).then_inc(wT_quant, 1)

            def scales(i0, i1, done):
                dve.wait_ge(f0_allmax, done)
                link(dve, dve_link, v.tensor_scalar(qsc[:, i0:i1], allmax[:, i0:i1], 1.0 / QMAX, 1e-12,
                                                    ALU.mult, ALU.max))
                v.reciprocal(qinv[:, i0:i1], qsc[:, i0:i1]).then_inc(f0_scale, 1)
                dve.wait_ge(f0_scale, done)

            def quantized(o, i, k):
                return v.tensor_scalar(o, i, -MAGIC, qsc[:, k:k + 1], ALU.add, ALU.mult)

            with dve.Fori(0, T) as t:
                v.bn_stats(f_stats[:, t, :], x[:, t, :]).then_inc(f0_stats, 1)
            dve.wait_ge(f0_stats, T)
            for t in range(T):
                v.bn_aggr(f_mv[:, t, :], f_stats[:, t, :]).then_inc(f0_mv, 1)
            dve.wait_ge(f0_rstd, 1)
            dve.wait_ge(wT_turned, 9)
            xm = x[:, :, :]
            link(dve, dve_link, v.tensor_tensor(xall, xm, f_mv[:, :, 0:1].broadcast_to([P, T, D]), ALU.subtract))
            link(dve, dve_link, v.tensor_tensor(xall, xall, f_rstd[:, :].unsqueeze(2).broadcast_to([P, T, D]), ALU.mult))
            v.tensor_reduce(pmax[:, QX:QX + 1], xall, AX.XY, ALU.max, apply_absolute_value=True).then_inc(f0_pmax, 1)
            scales(QX, QX + 1, 1)
            link(dve, dve_link, v.tensor_scalar(xall, xall, qinv[:, QX:QX + 1], MAGIC, ALU.mult, ALU.add))
            xab = xall.rearrange("p (b t) d -> p b t d", t=TPB)
            with dve.Fori(0, NB // 2) as i:
                for u in range(2):
                    b = 2 * i + u
                    dve.wait_ge(f0_xT, 1 + 2 * 2 * i)
                    quantized(xq[u], xab[:, b, :, :], QX).then_inc(f0_xq, 1)
                    for f in range(2 * NF0):
                        dve.wait_ge(f0_ugc, 1 + 2 * NF0 * b + f + 1)
                        v.tensor_reduce(amax[:, f, b, :], ug.rearrange("p f (b t) -> p f b t", t=BLK)[:, f, b, :], AX.X, ALU.max,
                                        apply_absolute_value=True).then_inc(f0_ugm, 1)
            dve.wait_ge(f0_ugm, 2 * NF0 * NB)
            v.tensor_reduce(pmax[:, QU:QG + 1], amax[:, :, :, :].rearrange("p (a f) b c -> p a (f b c)", a=2), AX.X, ALU.max)\
                .then_inc(f0_pmax, 1)
            scales(QU, QG + 1, 2)
            with dve.Fori(0, NF0 // 2) as i:
                for u in range(2):
                    f = 2 * i + u
                    g = ug[:, f + NF0, :]
                    dve.wait_ge(f0_gr, f + 1)
                    quantized(g, g, QG).then_inc(f0_gq, 1)
                for u in range(2):
                    f = 2 * i + u
                    g = ug[:, f + NF0, :]
                    dve.wait_ge(f0_sg, f + 1)
                    v.tensor_scalar(sg[u], sg[u], 65536.0, MAGIC, ALU.mult, ALU.add).then_inc(f0_sr, 1)
                    dve.wait_ge(f0_sr, 2 * f + 1)
                    v.tensor_scalar(sg[u], sg[u], -MAGIC, 65535.0, ALU.add, ALU.min).then_inc(f0_sr, 1)
                    dve.wait_ge(f0_sr, 2 * f + 2)
                    v.scalar_tensor_tensor(g, sg[u], 1.0 / 65536.0, g, ALU.mult, ALU.mult).then_inc(f0_g2, 1)
                    dve.wait_ge(f0_g2, 1 + f + 1)
                    v.tensor_reduce(amax[:, f, 0, :], g, AX.X, ALU.max, apply_absolute_value=True).then_inc(f0_ugm, 1)
            dve.wait_ge(f0_ugm, 2 * NF0 * NB + NF0)
            v.tensor_reduce(pmax[:, QS:QS + 1], amax[:, 0:NF0, 0, 0], AX.X, ALU.max).then_inc(f0_pmax, 1)
            scales(QS, QS + 1, 3)
            with dve.Fori(0, NF0) as f:
                g, up = ug[:, f + NF0, :], ug[:, f, :]
                dve.wait_ge(f0_g2r, f + 1)
                quantized(g, g, QS).then_inc(f0_g3, 1)
                dve.wait_ge(f0_ur, f + 1)
                quantized(up, up, QU).then_inc(f0_uq, 1)
                dve.wait_ge(f0_g3, f + 1)
                dve.wait_ge(f0_uq, f + 1)
                v.tensor_tensor(up, g, up, ALU.mult).then_inc(f0_o, 1)
                dve.wait_ge(f0_o, f + 1)
                v.tensor_reduce(amax[:, f, 1, :], up, AX.X, ALU.max, apply_absolute_value=True).then_inc(f0_ugm, 1)
            dve.wait_ge(f0_ugm, 2 * NF0 * NB + 2 * NF0)
            v.tensor_reduce(pmax[:, QO:QO + 1], amax[:, 0:NF0, 1, 0], AX.X, ALU.max).then_inc(f0_pmax, 1)
            scales(QO, QO + 1, 4)
            with dve.Fori(0, NB // 2) as i:
                for u in range(2):
                    b = 2 * i + u
                    for f in range(NF0):
                        dve.wait_ge(f0_or, NF0 * b + f + 1)
                        quantized(oq[u][:, f, :], oq[u][:, f, :], QO).then_inc(f0_oq, 1)
                    for t in range(TPB):
                        dve.wait_ge(f0_y, 1 + TPB * b + t + 1)
                        xt = x[:, :, :].rearrange("p (b t) d -> p b t d", t=TPB)[:, b, t, :]
                        v.tensor_tensor(xt, xt, ps[:, 4 * u + t, 0:D], ALU.add).then_inc(f0_x, 1)
            dve.wait_ge(f0_x, 1 + T)

            dve.wait_ge(c_vl_ps, 1)
            for g in range(G):
                r = v.tensor_tensor(c_vlm[0:NSEQ, g, :].rearrange("p (g e) -> p g e", g=G),
                                    ps[0:NSEQ, 3, 0:D].rearrange("p (g e) -> p g e", g=G),
                                    gmask[0:NSEQ, g, :].unsqueeze(2).broadcast_to([NSEQ, G, J * HD]), ALU.mult)
            r.then_inc(c_vl_done, 1)
            q_lane = qT_all.rearrange("p a (i l t) -> p a i l t", l=NL, t=P)
            with dve.Fori(0, NT) as i:
                for l in range(NL):
                    d_norm(None, l, i, i + 2 * NT)
                for l in range(NL):
                    d_scale(None, l, i, i + 2 * NT)
                for l in range(NL):
                    dve.wait_ge(s["q_evac"], tile(i, l))
                    for fo in range(KI):
                        r = v.tensor_scalar(q_lane[:, fo, i, l, :], bank[l][1][:, fo * P:(fo + 1) * P],
                                            colb[:, BQ1, fo:fo + 1], 0.25, ALU.add, ALU.mult)
                    r.then_inc(q_all, 1)

            def c_maxes(par, n):
                for g in range(G):
                    dve.wait_ge(c_s, G * n + g + 1)
                    v.tensor_reduce(c_nmx[par][:, g:g + 1], ps[:, g, 0:S], AX.X, ALU.max, negate=True)\
                        .then_inc(c_max, 1)

            def c_step(i, u, last):
                n = SPT * i + u
                dve.wait_ge(c_o, 1 + n)
                for k, bk in ((0, 6), (1, 4)):
                    dve.wait_ge(c_pt, 2 * n + k + 1)
                    v.tensor_copy(c_pT[:, 2 * k:2 * k + 2, :, :].rearrange("p g c t -> p (g c t)"), ps[:, bk, :])\
                        .then_inc(c_ptc, 1)
                dve.wait_ge(c_exp, 4 * n + 4)
                v.reciprocal(c_inv[:, :], c_sum[u % 2][:, :]).then_inc(c_rinv, 1)
                if not (last and u == SPT - 1):
                    c_maxes((u + 1) % 2, n + 1)
                dve.wait_ge(c_rinv, 1 + n + 1)
                v.tensor_tensor(c_rm[:, :, :], c_inv[:, :].unsqueeze(2).broadcast_to([P, G, J]),
                                mask4[:, :].unsqueeze(1).broadcast_to([P, G, J]), ALU.mult).then_inc(c_rmd, 1)
                dve.wait_ge(c_rmd, n + 1)
                dve.wait_ge(c_o, 1 + n + 1)
                dve.wait_ge(c_ot, 1 + n)
                v.tensor_tensor(c_om.rearrange("p g (j e) -> p g j e", e=HD),
                                ps[:, 7, 0:D].rearrange("p (g j e) -> p g j e", g=G, e=HD),
                                c_rm[:, :, :].unsqueeze(3).broadcast_to([P, G, J, HD]), ALU.mult).then_inc(c_omd, 1)
                dve.wait_ge(c_ot, 1 + n + 1)
                if u == 0:
                    dve.wait_ge(c_y, 1 + i)
                v.tensor_tensor(c_oT[:, :, u * L:(u + 1) * L],
                                ps[:, 7, D:D + KI * L].rearrange("p (a q) -> p a q", q=L),
                                colb[:, BV1, :].unsqueeze(2).broadcast_to([P, KI, L]), ALU.add).then_inc(c_otc, 1)
                if u == SPT - 1:
                    dve.wait_ge(c_y, 1 + i + 1)
                    v.tensor_tensor(x[:, i, :], x[:, i, :], ps[:, 5, 0:D], ALU.add).then_inc(c_x, 1)

            for l in range(NL):
                dve.wait_ge(q_all, 1 + tile(NT - 1, l))
                dve.wait_ge(s["x_biased"], tile(3 * NT - 1, l))
            c_maxes(0, 0)
            with dve.Fori(0, T - 1) as i:
                for u in range(SPT):
                    c_step(i, u, False)
            for u in range(SPT):
                c_step(T - 1, u, True)
            dve.wait_ge(c_x, T)
            for l in range(NL):
                v.memset(vbd[l], 0.0)
                v.memset(qs[l], 0.0)
                r = v.memset(ks[l], 0.0)
            r.then_inc(consts_made, 1)
            dve.wait_ge(consts_made, 2)
            attention(A1, [d_norm, d_scale, d_slots, d_queries] + common + [d_own, d_oT, d_add])
            for l in range(NL):
                dve.wait_ge(s["x_updated"], tile(3 * NT - 1, l))

            xb = x[:, :, :].rearrange("p (b t) d -> p b t d", t=TPB)

            def g_norm(b):
                for t in range(TPB):
                    v.bn_stats(g_stats[:, t, :], xb[:, b, t, :]).then_inc(g_st, 1)
                dve.wait_ge(g_st, TPB * b + TPB)
                stand(dve, "dve")
                for t in range(TPB):
                    v.bn_aggr(g_mv[:, t, :], g_stats[:, t, :]).then_inc(g_mvd, 1)
                dve.wait_ge(g_rs, b + 1)
                dve.wait_ge(g_xT, 1 + 2 * b)
                for t in range(TPB):
                    r = v.tensor_scalar(f_xn[:, t, :], xb[:, b, t, :], g_mv[:, t, 0:1], g_rstd[:, t:t + 1],
                                        ALU.subtract, ALU.mult)
                r.then_inc(g_xn, 1)

            def g_block(b, last):
                for o in range(NF1):
                    dve.wait_ge(g_sil, NF1 * b + o + 1)
                    v.scalar_tensor_tensor(f_ha[:, o, :], ps[:, 2 + o % 2, :], ffn_s[:, 1, o:o + 1],
                                           f_silu[:, o % 2, :], ALU.mult, ALU.mult).then_inc(g_h, 1)
                if not last:
                    g_norm(b + 1)
                for t in range(TPB):
                    dve.wait_ge(g_w3, TPB * b + t + 1)
                    v.tensor_tensor(f_y[:, t % 2, :], ps[:, RING3[t % 2], 0:D], w3s[:, :], ALU.mult).then_inc(g_ys, 1)
                    dve.wait_ge(g_ys, 1 + TPB * b + t + 1)
                    v.tensor_tensor(xb[:, b, t, :], xb[:, b, t, :], f_y[:, t % 2, :], ALU.add).then_inc(g_x, 1)

            g_norm(0)
            with dve.Fori(0, NB - 1) as b:
                g_block(b, False)
            g_block(NB - 1, True)

        @block.gpsimd
        def _(pool):
            p = nc.gpsimd

            def rsqrt(l, n):
                pool.wait_ge(s["mv_ready"], tile(n, l))
                stand(pool, "pool")
                p.tensor_scalar(vare[l][:, :], mv[l][:, 1:2], EPS, None, ALU.add).then_inc(s["vare_ready"], 1)
                pool.wait_ge(s["vare_ready"], tile(n, l))
                p.tensor_tensor(rstd[l][:, :], vare[l][:, :], minus_half[:, 0:1],
                                ALU.pow).then_inc(s["rstd_ready"], 1)

            def bias(l, i, n, k):
                pool.wait_ge(s["xn_ready"], tile(n, l))
                p.tensor_tensor(xl[:, i, l, :], xl[:, i, l, :], rowb[:, k, :], ALU.add)\
                    .then_inc(s["x_biased"], 1)

            pool.wait_ge(consts_made, 1)
            pool.wait_ge(in_const, 16 * N_CONST)
            for kind in (X0, A0):
                with pool.Fori(0, NT) as i:
                    for l in range(NL):
                        rsqrt(l, i + NORM[kind])
                    for l in range(NL):
                        bias(l, i, i + NORM[kind], BOUT[kind])
            pool.wait_ge(f0_mv, T)
            p.tensor_scalar(f_ve[:, :], f_mv[:, :, 1], EPS, None, ALU.add).then_inc(f0_ve, 1)
            pool.wait_ge(f0_ve, 1)
            p.tensor_tensor(f_rstd[:, :], f_ve[:, :], minus_half[:, 0:T], ALU.pow).then_inc(f0_rstd, 1)
            for k, (i0, i1) in enumerate(((QX, QX + 1), (QU, QG + 1), (QS, QS + 1), (QO, QO + 1))):
                pool.wait_ge(f0_pmax, k + 1)
                p.partition_all_reduce(allmax[:, i0:i1], pmax[:, i0:i1], P, bass.bass_isa.ReduceOp.max)\
                    .then_inc(f0_allmax, 1)
            pool.wait_ge(f0_x, 1 + T)
            with pool.Fori(0, NT) as i:
                for l in range(NL):
                    rsqrt(l, i + 2 * NT)
                for l in range(NL):
                    bias(l, i, i + 2 * NT, BO1)

            q_seq = qT_all.rearrange("p a (n q) -> p a n q", q=L)

            def c_query(par, n):
                q = q_seq[:, :, n, :].unsqueeze(2).broadcast_to([P, KI, 8, L])
                m = mask8[:, :].unsqueeze(1).unsqueeze(3).broadcast_to([P, KI, 8, L])
                p.tensor_tensor(c_qbd[par], q, m, ALU.mult).then_inc(c_q, 1)
                p.tensor_copy(c_kT[par][:, :, 2 * P:S], klast_seq[:, :, n, :]).then_inc(klast_copied, 1)

            for l in range(NL):
                pool.wait_ge(q_all, 1 + tile(NT - 1, l))
            pool.wait_ge(c_kl_done, 1)
            c_query(0, 0)
            c_query(1, 1)

            def c_step(i, u, last):
                if not (last and u >= 2):
                    n = SPT * i + u
                    pool.wait_ge(c_s, G * n + G)
                    c_query(u % 2, n + 2)

            with pool.Fori(0, T - 1) as i:
                for u in range(SPT):
                    c_step(i, u, False)
            for u in range(SPT):
                c_step(T - 1, u, True)
            pool.wait_ge(c_x, T)
            pool.wait_ge(consts_made, 2)
            pool.wait_ge(pl_scale_ready, 2)

            def lines(l, m):
                p1, p2 = pp[l][:, 0], pp[l][:, 1]
                pool.wait_ge(s["lines_in"], tile(m, l))
                pairs = ((0, 0, 1, 3), (3, 1, 2, 2), (5, 2, 3, 1))
                for dst, u, w in ((la[l], p1, p2), (lb[l], p2, p1)):
                    for at, pi, pj, k in pairs:
                        r = p.tensor_tensor(dst[:, :, at:at + k], u[:, :, pi:pi + 1].broadcast_to([P, H, k]),
                                            w[:, :, pj:pj + k], ALU.mult)
                r.then_inc(s["lines_step"], 1)
                pool.wait_ge(s["lines_step"], 4 * (NL * m + l) + 1)
                p.tensor_tensor(la[l][:, :, :], la[l][:, :, :], lb[l][:, :, :], ALU.subtract).then_inc(s["lines_step"], 1)
                pool.wait_ge(s["lines_step"], 4 * (NL * m + l) + 2)
                p.tensor_tensor(lb[l][:, :, :], la[l][:, :, :], la[l][:, :, :], ALU.mult).then_inc(s["lines_sq"], 1)
                pool.wait_ge(s["lines_sum"], 2 * (NL * m + l) + 2)
                p.tensor_tensor(lrn[l][:, :], lsq[l][:, :], minus_half[:, :], ALU.pow).then_inc(s["lines_step"], 1)
                pool.wait_ge(s["lines_step"], 4 * (NL * m + l) + 3)
                pool.wait_ge(s["q_evac"], tile(NT + m, l))
                p.tensor_tensor(la[l][:, :, :], la[l][:, :, :], lrn[l][:, :].unsqueeze(2).broadcast_to([P, H, NLINE]),
                                ALU.mult).then_inc(s["lines_step"], 1)
                pool.wait_ge(s["lines_step"], 4 * (NL * m + l) + 4)
                stand(pool, "pool")
                p.tensor_copy(qs[l][:, :, HD:HD + NLINE], la[l][:, :, :]).then_inc(s["q_slots"], 1)
                p.tensor_tensor(ks[l][:, :, HD:HD + NLINE], la[l][:, :, ::-1], plsc[:, :, :], ALU.mult)\
                    .then_inc(s["k_slots"], 1)

            with pool.Fori(0, NT) as i:
                for l in range(NL):
                    rsqrt(l, i + 3 * NT)
                for l in range(NL):
                    bias(l, i, i + 3 * NT, BOB)
                for l in range(NL):
                    lines(l, i)
            for l in range(NL):
                pool.wait_ge(s["x_updated"], tile(3 * NT - 1, l))

            def g_rsqrt(b):
                pool.wait_ge(g_mvd, TPB * b + TPB)
                stand(pool, "pool")
                p.tensor_scalar(g_ve[:, :], g_mv[:, :, 1], EPS, None, ALU.add).then_inc(g_ved, 1)
                pool.wait_ge(g_ved, b + 1)
                p.tensor_tensor(g_rstd[:, :], g_ve[:, :], minus_half[:, 0:TPB], ALU.pow).then_inc(g_rs, 1)

            with pool.Fori(0, NB) as b:
                g_rsqrt(b)


def kernel(**inputs):
    import numpy as np
    import concourse.bacc as bacc
    from concourse.bass_utils import run_bass_kernel_spmd

    a = {k: np.asarray(v) for k, v in inputs.items()}

    def cols(w):
        return np.ascontiguousarray(w.reshape(-1, P, w.shape[1]).transpose(1, 0, 2))

    def over(v):
        return np.ascontiguousarray(np.broadcast_to(v.reshape(1, -1), (P, v.size)))

    def rows(w):
        o, i = w.shape
        return np.ascontiguousarray(w.reshape(o // P, P, i).transpose(1, 0, 2).reshape(P, 48, 32))

    def feat(v):
        return v.reshape(KI, P).T

    ctxt = a["ctx_1024"]
    parts = np.arange(P)
    q = np.arange(L)
    delta = q[:, None] - q[None, :]
    visible = delta >= 0
    causal = np.where(visible, 0.0, -1e30).astype(np.float32)
    causal = np.broadcast_to(causal[None, :, None, :], (J, L, H, L)).reshape(P, H * L)
    pb = a["L0_attn_pos_bias"][np.where(visible, delta, 0)]
    pb = pb.reshape(L, L, G, J).transpose(3, 0, 2, 1)
    pb = np.broadcast_to(pb[:, :, :, None, :], (J, L, G, SPT, L)).reshape(P, H * L)
    bqkv0, bqkv1 = a["L0_attn_bqkv"], a["L1_attn_bqkv"]
    arrays = {
        "x": a["x"].reshape(T, P, D).transpose(1, 0, 2),
        "ident": np.eye(P, dtype=np.float32),
        "sel": (parts[:, None] % L == np.arange(L)).astype(np.float32),
        "mask8": (parts[:, None] // HD == np.arange(8)).astype(np.float32),
        "mask4": (parts[:, None] // L == np.arange(4)).astype(np.float32),
        "causal": causal,
        "posbias": pb,
        "gmask": np.broadcast_to(np.eye(G, dtype=np.float32), (P, G, G)),
        "colb": np.stack([feat(v) for v in (
            a["L0_xattn_bq"], a["L0_xattn_bk"], a["L0_xattn_bv"], bqkv0[0:D], bqkv0[D:2 * D], bqkv0[2 * D:],
            a["L0_attn_bgate"], a["L1_xattn_bq"], a["L1_xattn_bk"], a["L1_xattn_bv"])], axis=1),
        "rowb": np.stack([over(a[k]) for k in ("L0_xattn_bo", "L0_attn_bout", "L1_xattn_bo", "L1_attn_bout")],
                         axis=1),
        "a1_bv": feat(bqkv1[2 * D:]),
        "a1_bqk": over(bqkv1[0:2 * D]),
        "plscale": over(a["L1_attn_plucker_scale"]),
        "plsign": over(np.array([1, -1, 1, 1, -1, 1], np.float32)),
        "x0_wq": cols(a["L0_xattn_Wq"].T), "x0_wk": cols(a["L0_xattn_Wk"].T),
        "x0_wv": cols(a["L0_xattn_Wv"].T), "x0_wo": cols(a["L0_xattn_Wo"].T),
        "a0_wqkv": cols(a["L0_attn_Wqkv"]), "a0_wg": cols(a["L0_attn_Wgate"]), "a0_wout": cols(a["L0_attn_Wout"]),
        "w_up": rows(a["L0_ffn_w_up"]), "w_gate": rows(a["L0_ffn_w_gate"]), "w_down": rows(a["L0_ffn_w_down"]),
        "x1_wq": cols(a["L1_xattn_Wq"].T), "x1_wk": cols(a["L1_xattn_Wk"].T),
        "x1_wv": cols(a["L1_xattn_Wv"].T), "x1_wo": cols(a["L1_xattn_Wo"].T),
        "a1_wqkv": cols(a["L1_attn_Wqkv"]), "a1_wout": cols(a["L1_attn_Wout"]),
        "a1_wpl": np.stack([cols(a["L1_attn_W1p"]), cols(a["L1_attn_W2p"])], axis=2),
        "f_w1": cols(a["L1_ffn_w1_w"].T), "f_w2": cols(a["L1_ffn_w2_w"].T), "f_h1": cols(a["L1_ffn_h1_w"].T),
        "f_h2": cols(a["L1_ffn_h2_w"].T), "f_w3": cols(a["L1_ffn_w3_w"].T),
        "ffn_s": np.stack([a[f"L1_ffn_{k}_s"].reshape(NF1, P).T for k in ("w1", "w2", "h1", "h2")], axis=1),
        "w3s": over(a["L1_ffn_w3_s"]),
        "ctxT": ctxt.reshape(NSEQ, S, KI, P).transpose(0, 3, 2, 1),
        "ctx_last": ctxt[:, S - 1, :].reshape(NSEQ, KI, P).transpose(2, 1, 0),
        "ctxk": ctxt[:, 0:L, :].reshape(T, P, KI, P).transpose(3, 0, 2, 1),
    }
    arrays = {k: np.ascontiguousarray(v) for k, v in arrays.items()}
    nc = bacc.Bacc("TRN2", target_bir_lowering=False, num_devices=1)
    A = {k: nc.dram_tensor(f"in_{k}", v.shape, F32, kind="ExternalInput").ap() for k, v in arrays.items()}
    out = nc.dram_tensor("out", (P, T, D), F32, kind="ExternalOutput").ap()
    perceiver(nc, A, out)
    r = run_bass_kernel_spmd(nc, [{f"in_{k}": v for k, v in arrays.items()}], core_ids=[0])
    got = np.asarray(r.results[0]["out"])
    return np.ascontiguousarray(got.transpose(1, 0, 2)).reshape(NSEQ, L, D)
```

```python
import concourse.bass as bass
from concourse import mybir
from contextlib import ExitStack

F32 = mybir.dt.float32
ALU = mybir.AluOpType
ACT = mybir.ActivationFunctionType
AX = mybir.AxisListType

P = 128
D = 256
KI = D // P
NSEQ = 64
L = 32
S = 257
T = NSEQ * L // P
SPT = P // L
H = 16
HD = D // H
G = 4
J = H // G
NL = 4
NT = T // NL
F0 = 768
NF0 = F0 // P
F1 = 1024
NF1 = F1 // P
BLK = 512
NB = NSEQ * L // BLK
TPB = BLK // P
EPS = 1e-5
MAGIC = 12582912.0
QMAX = 32767.0
NLINE = 6
SLOT = 32


def perceiver(nc, A, out):
    ctx = ExitStack()
    with ctx:
        def sb(name, shape, dt=F32):
            return ctx.enter_context(nc.sbuf_tensor(name, shape, dt))

        def sem(name):
            return ctx.enter_context(nc.semaphore(name))

        def lanes(name):
            return [sem(f"{name}{l}") for l in range(NL)]

        x = sb("x", [P, T, D])
        ident = sb("ident", [P, P])
        sel = sb("sel", [P, L])
        mask8 = sb("mask8", [P, 8])
        mask4 = sb("mask4", [P, 4])
        causal = sb("causal", [P, H * L])
        posmask = sb("posmask", [P, H * L])
        minus_half = sb("minus_half", [P, H])
        x1_wq, x1_wk, x1_wv, x1_wo = (sb(f"x1_w{c}", [P, KI, D]) for c in "qkvo")
        a1_wqkv = sb("a1_wqkv", [P, KI, 3 * D])
        a1_wpl = sb("a1_wpl", [P, KI, 2, 4 * H])
        a1_wout = sb("a1_wout", [P, KI, D])
        colb = sb("colb", [P, 10, KI])
        BQ0, BK0, BV0, BQA, BKA, BVA, BG, BQ1, BK1, BV1 = range(10)
        a1_bv = sb("a1_bv", [P, KI])
        nbg = sb("nbg", [P, KI])
        rowb = sb("rowb", [P, 4, D])
        BO0, BOA, BO1, BOB = range(4)
        a1_bqk = sb("a1_bqk", [P, 2 * D])
        plsc = sb("plsc", [P, H, NLINE])
        plscale = sb("plscale", [P, H])
        plsign = sb("plsign", [P, NLINE])
        ffn_s = sb("ffn_s", [P, 4, NF1])
        w3s = sb("w3s", [P, D])

        LANE = 5888
        R1 = NL * LANE
        W0 = 2 * F0 // P * NSEQ * L
        RSIZE = W0 + 2 * 4608 + T * D + 1536
        R = sb("R", [P, RSIZE])

        def view(at, *shape):
            size = 1
            for s in shape:
                size *= s
            assert at + size <= RSIZE
            v = R[:, at:at + size]
            if len(shape) == 2:
                v = v.rearrange("p (a b) -> p a b", b=shape[1])
            elif len(shape) == 3:
                v = v.rearrange("p (a b c) -> p a b c", b=shape[1], c=shape[2])
            elif len(shape) == 4:
                v = v.rearrange("p (a b c d) -> p a b c d", b=shape[1], c=shape[2], d=shape[3])
            return v

        def put(at, sizes):
            places = []
            for s in sizes:
                places.append(at)
                at += s
            return places

        lane_at = [put(l * LANE, [256, 256, 2048, 512, 1024, 512, 256, 256, 256, 512]) for l in range(NL)]
        xn = [view(a[0], D) for a in lane_at]
        oT = [view(a[0], KI, P) for a in lane_at]
        xnT = [view(a[1], KI, P) for a in lane_at]
        qbd = [view(a[2], 2048) for a in lane_at]
        om = [view(a[2], KI * SPT * P) for a in lane_at]
        kT = [view(a[3], 512) for a in lane_at]
        pT = [view(a[3], G, P) for a in lane_at]
        vbd = [view(a[4], SPT, D) for a in lane_at]
        sc = [view(a[5], H, L) for a in lane_at]
        pr = [view(a[5], G, P) for a in lane_at]
        gT = [view(a[6], KI, P) for a in lane_at]
        ctxk = [view(a[7], KI, P) for a in lane_at]
        qT = [view(a[8], D) for a in lane_at]
        qs = [view(a[7], H, SLOT) for a in lane_at]
        ks = [view(a[9], H, SLOT) for a in lane_at]

        stats = [sb(f"stats{l}", [P, 6]) for l in range(NL)]
        mv = [sb(f"mv{l}", [P, 2]) for l in range(NL)]
        vare = [sb(f"vare{l}", [P, 1]) for l in range(NL)]
        rstd = [sb(f"rstd{l}", [P, 1]) for l in range(NL)]
        nmx = [sb(f"nmx{l}", [P, H]) for l in range(NL)]
        rsum = [sb(f"rsum{l}", [P, H]) for l in range(NL)]
        rinv = [sb(f"rinv{l}", [P, H]) for l in range(NL)]
        rm = [sb(f"rm{l}", [P, H, J]) for l in range(NL)]
        line_at = [put(RSIZE - 320 * (l + 1), [128, 96, 96]) for l in range(NL)]
        pp = [view(a[0], 2, H, 4) for a in line_at]
        la = [view(a[1], H, NLINE) for a in line_at]
        lb = [view(a[2], H, NLINE) for a in line_at]
        lsq = [sb(f"lsq{l}", [P, H]) for l in range(NL)]
        lrn = [sb(f"lrn{l}", [P, H]) for l in range(NL)]

        a = put(W0, [512] * 4 + [1536, 512, 512])
        x0_wq, x0_wk, x0_wv, x0_wo = (view(a[i], KI, D) for i in range(4))
        a0_wqkv, a0_wg, a0_wout = view(a[4], KI, 3 * D), view(a[5], KI, D), view(a[6], KI, D)
        XN = a[6] + 512
        WT = XN + T * D
        wuT, wgT, wdT = view(WT, KI, F0), view(WT + 1536, KI, F0), view(WT + 3072, NF0, D)
        w_nat = [view(XN, 48, 32), view(XN + 1536, 48, 32), view(WT + 4608, 48, 32)]
        ug = view(0, 2 * NF0, NSEQ * L)
        xall = view(XN, T, D)
        xq = [view(W0 + i * 1024, TPB, D) for i in range(2)]
        xqT = [view(W0 + 2048 + i * 1024, KI, BLK) for i in range(2)]
        sg = [view(at, 2048) for at in (XN, XN + 2048, W0, W0 + 2048)]
        oq = [view(W0 + i * 3072, NF0, BLK) for i in range(2)]
        f_stats = sb("f_stats", [P, T, 6])
        f_mv = sb("f_mv", [P, T, 2])
        f_ve = sb("f_ve", [P, T])
        f_rstd = sb("f_rstd", [P, T])
        wmax = sb("wmax", [P, 3, 48, 1])
        wsc = sb("wsc", [P, 3, 48, 1])
        winv = sb("winv", [P, 3, 48, 1])
        W_PART = [P, 48 // NT, 32]
        f_stats4 = f_stats.rearrange("p (i l) c -> p i l c", l=NL)
        amax = sb("amax", [P, 2 * NF0, NB, 1])
        pmax = sb("pmax", [P, 5])
        allmax = sb("allmax", [P, 5])
        qsc = sb("qsc", [P, 5])
        qinv = sb("qinv", [P, 5])
        QX, QU, QG, QS, QO = range(5)

        a = put(512, [KI * NSEQ * L, 1024])
        assert a[-1] + 1024 <= LANE
        qT_all = view(a[0], KI, NSEQ * L)
        c_qbd = [view(a[1] + i * 512, KI, 8, L) for i in range(2)]
        a = put(LANE + 512, [2 * KI * S, 2 * KI * S, 1024, 512, G * S])
        assert a[-1] + G * S <= 2 * LANE
        c_ctx = [view(a[0] + i * KI * S, KI, S) for i in range(2)]
        c_kT = [view(a[1] + i * KI * S, KI, S) for i in range(2)]
        c_v = [view(a[2] + i * 512, 2, D) for i in range(2)]
        c_vl = [view(a[3] + i * 256, D) for i in range(2)]
        c_p = view(a[4], G, S)
        a = put(2 * LANE + 512, [1024, 256, 256, 128, 128, 256, 256])
        assert a[-1] + 256 <= 3 * LANE
        c_pT = view(a[0], 4, 2, P)
        c_om = view(a[1], G, J * HD)
        c_oT = view(a[2], KI, P)
        c_last = view(a[3], KI, NSEQ)
        c_klast = view(a[4], KI, NSEQ)
        klast_seq = c_klast.rearrange("p a (n c) -> p a n c", c=1)
        c_vlast = view(a[5], D)
        c_osum = view(a[6], G, J * HD)
        c_nmx = [sb(f"c_nmx{i}", [P, G]) for i in range(2)]
        c_sum = [sb(f"c_sum{i}", [P, G]) for i in range(2)]
        c_inv = sb("c_inv", [P, G])
        c_rm = sb("c_rm", [P, G, J])
        vl_dram = nc.dram_tensor("vl_dram", [NSEQ, D], F32, kind="Internal").ap()

        a = put(R1, [KI * F1, KI * F1, NF1 * F1])
        f_w1, f_w2 = view(a[0], KI, F1), view(a[1], KI, F1)
        f_h1 = view(a[2], NF1, F1)
        a = put(0, [1024, 1024, 4096, 4096, 1024, 512, NF1 * F1, NF1 * D])
        assert a[-1] + NF1 * D <= R1
        f_xn, f_xnT = view(a[0], TPB, D), view(a[1], KI, BLK)
        f_ha, f_hb = view(a[2], NF1, BLK), view(a[3], NF1, BLK)
        f_silu = view(a[4], 2, BLK)
        f_y = view(a[5], 2, D)
        f_h2, f_w3 = view(a[6], NF1, F1), view(a[7], NF1, D)
        g_stats = sb("g_stats", [P, TPB, 6])
        g_mv = sb("g_mv", [P, TPB, 2])
        g_ve = sb("g_ve", [P, TPB])
        g_rstd = sb("g_rstd", [P, TPB])

        magic = sb("magic", [P, 1])
        unmagic = sb("unmagic", [P, 1])

        ps = ctx.enter_context(nc.psum_tensor("ps", [P, 8, 512], F32))

        in_const, in_later_const = sem("in_const"), sem("in_later_const")
        in_x = sem("in_x")
        in_w = {k: sem(f"in_w_{k}") for k in ("x0", "a0", "nat", "x1", "a1", "ffn", "ffn2")}
        posmask_ready, gate_bias_ready, pl_scale_ready, consts_made = map(
            sem, ("posmask_ready", "gate_bias_ready", "pl_scale_ready", "consts_made"))
        ctxk_in = lanes("ctxk_in")
        names = ("stats_ready mv_ready vare_ready rstd_ready xn_ready xnT_ready xnT_copied x_biased "
                 "qk_ready v_ready q_masked k_copied v_spread scores_ready scores_masked max_ready scores_shifted "
                 "probs_ready sum_ready pT_ready pT_copied o_ready o_normed oT_ready oT_copied "
                 "gate_exp gate_plus gate_done y_ready x_updated "
                 "lines_in lines_mul lines_step lines_sq lines_sum q_slots k_slots "
                 "qk_slots_ready q_evac q_copied").split()
        s = {n: sem(n) for n in names}


        def tile(n, l):
            return NL * n + l + 1

        dve_link = sem("dve_link")
        passed = {e: sem(f"{e}_passed") for e in ("act", "dve", "pool")}

        def stand(eng, e):
            eng.sem_inc(passed[e], 1)
        links = {}

        def link(eng, chain, ins):
            links[chain] = links.get(chain, 0) + 1
            ins.then_inc(chain, 1)
            eng.wait_ge(chain, links[chain])

        w_max, w_scale, w_inverse, w_divided, w_rounded = map(
            sem, ("w_max", "w_scale", "w_inverse", "w_divided", "w_rounded"))
        wT_quant, wT_turned, wT_copied = sem("wT_quant"), sem("wT_turned"), sem("wT_copied")
        f0_stats, f0_mv, f0_ve, f0_rstd, f0_pmax, f0_allmax, f0_scale = map(
            sem, ("f0_stats", "f0_mv", "f0_ve", "f0_rstd", "f0_pmax", "f0_allmax", "f0_scale"))
        f0_xq, f0_xT, f0_xTc, f0_ug, f0_ugc, f0_ugm = map(
            sem, ("f0_xq", "f0_xT", "f0_xTc", "f0_ug", "f0_ugc", "f0_ugm"))
        f0_gr, f0_gq, f0_sg, f0_sr_act, f0_sr_pool, f0_g2, f0_g2r, f0_ur, f0_sgr, f0_uq, f0_o = map(
            sem, ("f0_gr", "f0_gq", "f0_sg", "f0_sr_act", "f0_sr_pool", "f0_g2", "f0_g2r", "f0_ur", "f0_sgr", "f0_uq", "f0_o"))
        f0_or, f0_oq, f0_y, f0_x = map(sem, ("f0_or", "f0_oq", "f0_y", "f0_x"))

        c_last_in, c_kl_ps, c_kl_done, c_vl_ps, c_vl_done, c_vl_out = map(
            sem, ("c_last_in", "c_kl_ps", "c_kl_done", "c_vl_ps", "c_vl_done", "c_vl_out"))
        q_all = sem("q_all")
        ctx_in = [sem(f"ctx_in{i}") for i in range(2)]
        vl_in = [sem(f"vl_in{i}") for i in range(2)]
        (k_ready, k_copied, klast_copied, v_ready, v_copied, c_q, c_s, c_max, c_exp, c_pt, c_ptc, c_lastk, c_added,
         c_o, c_rinv, c_rmd, c_omd, c_ot, c_otc, c_y, c_x) = map(sem, (
             "c_k_ready", "c_k_copied", "c_klast_copied", "c_v_ready", "c_v_copied", "c_q", "c_s", "c_max", "c_exp",
             "c_pt", "c_ptc", "c_lastk", "c_added", "c_o", "c_rinv", "c_rmd", "c_omd", "c_ot", "c_otc", "c_y", "c_x"))
        (g_st, g_mvd, g_ved, g_rs, g_xn, g_xT, g_xTc, g_ab, g_sil, g_h, g_h1, g_ge1, g_h2, g_ge2, g_w3, g_ys,
         g_x, g_out) = map(sem, ("g_st", "g_mvd", "g_ved", "g_rs", "g_xn", "g_xT", "g_xTc", "g_ab", "g_sil",
                                 "g_h", "g_h1", "g_ge1", "g_h2", "g_ge2", "g_w3", "g_ys", "g_x", "g_out"))

        free = {"act": (f0_xTc, f0_ugc, g_ge2), "dve": (f0_x, f0_g2, q_all, c_otc, c_rinv, g_ys),
                "pe": (f0_ug, f0_y, f0_xT, c_o, c_ot, c_y, g_xT), "pool": (c_lastk,)}

        RING1, RING2, RING3 = (4, 5, 0, 1), (2, 3, 4, 5), (0, 1)

        block = ctx.enter_context(nc.Block())

        X0, A0, A1 = "x0", "a0", "a1"
        SLOTS0, SLOTS1 = 20, 24

        def run_lanes(eng, slots, stages):
            lag = slots // NL

            def a_round(i, steps, i_behind, steps_behind):
                for slot in range(slots):
                    for l in sorted(range(NL), key=lambda l: -((slot - lag * l) % slots)):
                        of_round, n = (steps_behind, i_behind) if slot < lag * l else (steps, i)
                        for at, step in of_round:
                            if at == (slot - lag * l) % slots:
                                step(l, n)

            behind = ()
            for enter, steps in stages:
                enter()
                a_round(0, steps, NT - 1, behind)
                with eng.Fori(1, NT) as i:
                    a_round(i, steps, i - 1, steps)
                behind = steps
            a_round(NT, (), NT - 1, behind)

        BASE = {X0: 0, A0: NT, A1: 2 * NT}
        NORM = {X0: 0, A0: NT, A1: 3 * NT}
        WOUT = {X0: x0_wo, A0: a0_wout, A1: a1_wout}
        BOUT = {X0: BO0, A0: BOA, A1: BOB}
        BIAS_Q = {X0: BQ0, A0: BQA}
        BIAS_K = {X0: BK0, A0: BKA}
        BIAS_V = {X0: colb[:, BV0, :], A0: colb[:, BVA, :], A1: a1_bv[:, :]}
        N_CONST, N_LATER_CONST = 7, 6
        xl = x[:, :, :].rearrange("p (i l) d -> p i l d", l=NL)
        bank = [[ps[:, 2 * l + i, :] for i in range(2)] for l in range(NL)]

        def halves(ap):
            return ap.rearrange("p (a b) -> p a b", b=P)

        @block.sync
        def _(sp):
            sp.dma_start(x[:, 0:2, :], A["x"][:, 0:2, :]).then_inc(in_x, 16)
            for d, n in ((ident, "ident"), (sel, "sel"), (mask8, "mask8"), (mask4, "mask4"), (causal, "causal"),
                         (colb, "colb"), (rowb, "rowb")):
                sp.dma_start(d[:], A[n]).then_inc(in_const, 16)
            for d, n in ((x0_wq, "x0_wq"), (x0_wk, "x0_wk"), (x0_wv, "x0_wv"), (x0_wo, "x0_wo")):
                sp.dma_start(d, A[n]).then_inc(in_w["x0"], 16)

            def load_ctxk(l, i):
                sp.dma_start(ctxk[l], A["ctxk"][:, NL * i + l]).then_inc(ctxk_in[l], 16)

            for l in range(NL):
                load_ctxk(l, 0)
            sp.dma_start(x[:, 2:T, :], A["x"][:, 2:T, :]).then_inc(in_x, 16)
            for d, n in ((posmask, "posbias"), (a1_bv, "a1_bv"), (a1_bqk, "a1_bqk"), (plscale, "plscale"),
                         (plsign, "plsign"), (w3s, "w3s")):
                sp.dma_start(d[:], A[n]).then_inc(in_later_const, 16)
            for d, n in ((a0_wqkv, "a0_wqkv"), (a0_wg, "a0_wg"), (a0_wout, "a0_wout")):
                sp.dma_start(d, A[n]).then_inc(in_w["a0"], 16)
            for d, n in zip(w_nat, ("w_up", "w_gate", "w_down")):
                sp.dma_start(d, A[n]).then_inc(in_w["nat"], 16)
            for d, n in ((x1_wq, "x1_wq"), (x1_wk, "x1_wk"), (x1_wv, "x1_wv"), (x1_wo, "x1_wo")):
                sp.dma_start(d[:], A[n]).then_inc(in_w["x1"], 16)
            for d, n in ((a1_wqkv, "a1_wqkv"), (a1_wpl, "a1_wpl"), (a1_wout, "a1_wout"), (ffn_s, "ffn_s")):
                sp.dma_start(d[:], A[n]).then_inc(in_w["a1"], 16)
            with sp.Fori(1, NT) as i:
                for l in range(NL):
                    sp.wait_ge(s["v_ready"], tile(i - 1, l))
                    load_ctxk(l, i)

            sp.wait_ge(f0_x, 1 + T)
            sp.dma_start(c_last, A["ctx_last"]).then_inc(c_last_in, 16)
            for n in range(2):
                sp.dma_start(c_ctx[n], A["ctxT"][n]).then_inc(ctx_in[n], 16)
            for d, n in ((f_w1, "f_w1"), (f_w2, "f_w2"), (f_h1, "f_h1")):
                sp.dma_start(d, A[n]).then_inc(in_w["ffn"], 16)
            sp.wait_ge(c_vl_done, 1)
            sp.dma_start(vl_dram, c_vlast[0:NSEQ, :]).then_inc(c_vl_out, 16)
            sp.wait_ge(c_vl_out, 16)
            sp.dma_start(c_vl[0], vl_dram[0].unsqueeze(0).broadcast_to([P, D])).then_inc(vl_in[0], 16)

            def c_loads(i, last):
                for u in range(SPT):
                    n = SPT * i + u
                    if not (last and u == SPT - 1):
                        if not (isinstance(i, int) and n == 0):
                            sp.wait_ge(c_lastk, 1 + n)
                        sp.dma_start(c_vl[(u + 1) % 2], vl_dram[n + 1].unsqueeze(0).broadcast_to([P, D]))\
                            .then_inc(vl_in[(u + 1) % 2], 16)
                    if not (last and u >= 2):
                        sp.wait_ge(v_ready, n + 1)
                        sp.dma_start(c_ctx[u % 2], A["ctxT"][n + 2]).then_inc(ctx_in[u % 2], 16)

            with sp.Fori(0, T - 1) as i:
                c_loads(i, False)
            c_loads(T - 1, True)
            sp.wait_ge(s["x_updated"], tile(3 * NT - 1, NL - 1))
            for d, n in ((f_h2, "f_h2"), (f_w3, "f_w3")):
                sp.dma_start(d, A[n]).then_inc(in_w["ffn2"], 16)
            for b in range(NB):
                sp.wait_ge(g_x, TPB * (b + 1))
                sp.dma_start(out[:, TPB * b:TPB * (b + 1), :], x[:, TPB * b:TPB * (b + 1), :]).then_inc(g_out, 16)
            sp.wait_ge(g_out, 16 * NB)

        @block.tensor
        def _(pe):
            for m in free["pe"]:
                pe.sem_inc(m, 1)
            mm = nc.tensor.matmul
            tr = nc.tensor.transpose

            def project(dst, w, src, fo):
                for ki in range(KI):
                    r = mm(dst, w[:, ki, fo * P:(fo + 1) * P], src[:, ki, :], start=(ki == 0), stop=(ki == KI - 1))
                return r

            def project_rows(dst, src, w):
                for ki in range(KI):
                    r = mm(dst, src[:, ki, :], w[:, ki], start=(ki == 0), stop=(ki == KI - 1))
                return r

            def p_turn(kind, l, n):
                pe.wait_ge(s["xn_ready"], tile(n, l))
                for ki in range(KI):
                    r = tr(halves(bank[l][0])[:, ki, :], xn[l][:, ki * P:(ki + 1) * P], ident[:])
                r.then_inc(s["xnT_ready"], 1)

            def p_project(kind, l, n):
                pe.wait_ge(s["xnT_copied"], tile(n - BASE[kind] + NORM[kind], l))
                qk = bank[l][0].rearrange("p (a b) -> p a b", b=P)
                if kind == A1:
                    project_rows(bank[l][0], xnT[l], a1_wqkv[:, :, 0:2 * D]).then_inc(s["qk_ready"], 1)
                    project_rows(bank[l][1][:, D:D + 8 * H], xnT[l],
                                 a1_wpl[:, :, :, :].rearrange("p k a b -> p k (a b)"))
                    project_rows(bank[l][1][:, 0:D], xnT[l], a1_wqkv[:, :, 2 * D:3 * D]).then_inc(s["v_ready"], 1)
                    return
                wq = x0_wq if kind == X0 else a0_wqkv[:, :, 0:D]
                wk = x0_wk if kind == X0 else a0_wqkv[:, :, D:2 * D]
                wv = x0_wv if kind == X0 else a0_wqkv[:, :, 2 * D:3 * D]
                src = ctxk[l] if kind == X0 else xnT[l]
                for fo in range(KI):
                    project(qk[:, fo, :], wq, xnT[l], fo)
                if kind == X0:
                    pe.wait_ge(ctxk_in[l], 16 * (n + 1))
                for fo in range(KI):
                    r = project(qk[:, KI + fo, :], wk, src, fo)
                r.then_inc(s["qk_ready"], 1)
                if kind == A0:
                    for fo in range(KI):
                        project(halves(bank[l][1])[:, KI + fo, :], a0_wg, xnT[l], fo)
                project_rows(bank[l][1][:, 0:D], src, wv).then_inc(s["v_ready"], 1)

            def p_slots(kind, l, n):
                pe.wait_ge(s["q_slots"], tile(n - BASE[A1], l))
                for g in range(G):
                    r = tr(bank[l][0][:, g * P:(g + 1) * P], qs[l][:, J * g:J * (g + 1), :], ident[:])
                pe.wait_ge(s["k_slots"], tile(n - BASE[A1], l))
                pe.wait_ge(s["v_spread"], tile(n, l))
                for g in range(G):
                    r = tr(bank[l][1][:, g * P:(g + 1) * P], ks[l][:, J * g:J * (g + 1), :], ident[:])
                r.then_inc(s["qk_slots_ready"], 1)

            def p_scores(kind, l, n):
                pe.wait_ge(s["q_masked"], tile(n, l))
                pe.wait_ge(s["k_copied"], tile(n, l))
                for g in range(G):
                    for b in range(SPT):
                        if kind == A1:
                            q = qbd[l][:, (g * SPT + b) * P:(g * SPT + b + 1) * P]
                            k = kT[l][:, g * P + b * L:g * P + (b + 1) * L]
                        else:
                            at = (((g // 2) * SPT + b) * 2 + g % 2) * P
                            q = qbd[l][:, at:at + P]
                            k = kT[l][:, (g // 2) * P + b * L:(g // 2) * P + (b + 1) * L]
                        r = mm(bank[l][0][:, g * P + b * L:g * P + (b + 1) * L], q, k, start=True, stop=True)
                r.then_inc(s["scores_ready"], 1)

            def p_turn_probs(kind, l, n):
                pe.wait_ge(s["probs_ready"], tile(n, l))
                for g in range(G):
                    r = tr(bank[l][1][:, g * P:(g + 1) * P], pr[l][:, g, :], ident[:])
                r.then_inc(s["pT_ready"], 1)

            def p_values(kind, l, n):
                pe.wait_ge(s["v_spread"], tile(n, l))
                pe.wait_ge(s["pT_copied"], tile(n, l))
                for g in range(G):
                    o = bank[l][g // 2].rearrange("p (b g e) -> p b g e", g=2, e=J * HD)[:, :, g % 2, :]
                    r = mm(o, pT[l][:, g, :], vbd[l][:, :, g * J * HD:(g + 1) * J * HD], start=True, stop=True)
                r.then_inc(s["o_ready"], 1)

            def p_gather(kind, l, n):
                pe.wait_ge(s["o_normed"], tile(n, l))
                for half in range(KI):
                    for b in range(SPT):
                        r = mm(bank[l][0][:, D + half * P + b * L:D + half * P + (b + 1) * L],
                               om[l][:, (half * SPT + b) * P:(half * SPT + b + 1) * P], sel[:], start=True, stop=True)
                r.then_inc(s["oT_ready"], 1)

            def p_out(kind, l, n):
                pe.wait_ge(s["oT_copied"], tile(n, l))
                project_rows(bank[l][1][:, 0:D], oT[l], WOUT[kind]).then_inc(s["y_ready"], 1)

            pe.wait_ge(in_const, 16 * N_CONST)

            WEIGHTS = {"x0": 4, "a0": 3, "a1": 4}

            def attention(kind, w, steps):
                return (lambda: pe.wait_ge(in_w[w], 16 * WEIGHTS[w]),
                        [(at, lambda l, i, step=step: step(kind, l, i + (NORM if step is p_turn else BASE)[kind]))
                         for at, step in steps])

            steps_x0 = [(2, p_turn), (4, p_project), (7, p_scores), (10, p_turn_probs), (12, p_values), (14, p_gather),
                     (16, p_out)]
            steps_a0 = [(2, p_turn), (3, p_project), (5, p_scores), (8, p_turn_probs), (10, p_values), (12, p_gather),
                     (14, p_out)]
            run_lanes(pe, SLOTS0, [attention(X0, "x0", steps_x0), attention(A0, "a0", steps_a0)])

            for l in range(NL):
                pe.wait_ge(s["x_updated"], tile(2 * NT - 1, l))
            k = 0
            for m in range(3):
                pe.wait_ge(wT_quant, 3 * NT)
                w = w_nat[m].rearrange("p a b -> p (a b)")
                a_n, b_n = (NF0, KI) if m < 2 else (KI, NF0)
                for bi in range(b_n):
                    for ai in range(a_n):
                        at = (bi * a_n + ai) * P
                        if k % 4 == 0 and k // 4 >= 8:
                            pe.wait_ge(wT_copied, k // 4 - 7)
                        r = tr(ps[:, (k // 4) % 8, (k % 4) * P:(k % 4 + 1) * P],
                               w[:, (ai * b_n + bi) * P:(ai * b_n + bi + 1) * P], ident[:])
                        k += 1
                        if k % 4 == 0:
                            r.then_inc(wT_turned, 1)
            pe.wait_ge(wT_copied, 9)

            with pe.Fori(0, NB // 2) as i:
                for u in range(2):
                    b = 2 * i + u
                    pe.wait_ge(f0_xq, b + 1)
                    pe.wait_ge(f0_xTc, 1 + 2 * b)
                    for ki in range(KI):
                        for t in range(TPB):
                            r = tr(ps[:, 6 + ki, t * P:(t + 1) * P], xq[u][:, t, ki * P:(ki + 1) * P], ident[:])
                        r.then_inc(f0_xT, 1)
                    pe.wait_ge(f0_xTc, 1 + 2 * b + 2)
                    for f in range(2 * NF0):
                        w = wuT if f < NF0 else wgT
                        fb = ps[:, f % 4, :]
                        if f >= 4:
                            pe.wait_ge(f0_ugc, 1 + 2 * NF0 * b + f - 3)
                        else:
                            pe.wait_ge(f0_ugc, 1 + 2 * NF0 * b)
                        project(fb, w, xqT[u], f % NF0).then_inc(f0_ug, 1)
            with pe.Fori(0, NB // 2) as i:
                for u in range(2):
                    b = 2 * i + u
                    pe.wait_ge(f0_oq, NF0 * (b + 1))
                    pe.wait_ge(f0_x, 1 + TPB * 2 * i)
                    for t in range(TPB):
                        for f in range(NF0):
                            r = mm(ps[:, 4 * u + t, 0:D], oq[u][:, f, t * P:(t + 1) * P], wdT[:, f, :],
                                   start=(f == 0), stop=(f == NF0 - 1))
                        r.then_inc(f0_y, 1)

            pe.wait_ge(f0_x, 1 + T)
            pe.wait_ge(in_w["x1"], 64)
            pe.wait_ge(c_last_in, 16)
            for fo in range(KI):
                r = project(ps[:, 2, fo * NSEQ:(fo + 1) * NSEQ], x1_wk, c_last, fo)
            r.then_inc(c_kl_ps, 1)
            project_rows(ps[0:NSEQ, 3, 0:D], c_last, x1_wv).then_inc(c_vl_ps, 1)
            pe.wait_ge(c_kl_done, 1)
            pe.wait_ge(c_vl_done, 1)
            with pe.Fori(0, NT) as i:
                for l in range(NL):
                    p_turn(None, l, i + 2 * NT)
                for l in range(NL):
                    pe.wait_ge(s["xnT_copied"], tile(i + 2 * NT, l))
                    pe.wait_ge(q_all, 1 + NL * i)
                    for fo in range(KI):
                        r = project(bank[l][1][:, fo * P:(fo + 1) * P], x1_wq, xnT[l], fo)
                    r.then_inc(s["q_evac"], 1)

            kb, vb, tb, ob = (ps[:, i, :] for i in (4, 5, 6, 7))
            o_all = ob[:, 0:D].rearrange("p (g e) -> p g e", g=G)

            def c_keys(par):
                for fo in range(KI):
                    for ki in range(KI):
                        r = mm(kb[:, fo * D:(fo + 1) * D], x1_wk[:, ki, fo * P:(fo + 1) * P],
                               c_ctx[par][:, ki, 0:2 * P], start=(ki == 0), stop=(ki == KI - 1))
                r.then_inc(k_ready, 1)

            def c_values(par):
                for c in range(2):
                    for ki in range(KI):
                        r = mm(vb[:, c * D:(c + 1) * D], c_ctx[par][:, ki, c * P:(c + 1) * P], x1_wv[:, ki, :],
                               start=(ki == 0), stop=(ki == KI - 1))
                r.then_inc(v_ready, 1)

            def c_scores(par):
                for g in range(G):
                    mm(ps[:, g, 0:S], c_qbd[par][:, g // 2, J * (g % 2):J * (g % 2 + 1), :], c_kT[par][:, g // 2, :],
                       start=True, stop=True).then_inc(c_s, 1)

            def c_step(i, u, last):
                n = SPT * i + u
                par = u % 2
                pe.wait_ge(c_exp, 4 * n + 4)
                for g in range(G):
                    if g == 2:
                        if not (last and u == SPT - 1):
                            pe.wait_ge(k_copied, n + 2)
                    dst = tb if g < 2 else kb
                    for c in range(2):
                        at = ((g % 2) * 2 + c) * P
                        r = tr(dst[:, at:at + P], c_p[:, g, c * P:(c + 1) * P], ident[:])
                    if g % 2:
                        r.then_inc(c_pt, 1)
                if not (last and u == SPT - 1):
                    pe.wait_ge(klast_copied, n + 2)
                    pe.wait_ge(c_q, n + 2)
                    c_scores((u + 1) % 2)
                pe.wait_ge(c_otc, 1 + n)
                pe.wait_ge(v_copied, n + 1)
                for g in range(G):
                    if g % 2 == 0:
                        pe.wait_ge(c_ptc, 2 * n + 1 + g // 2)
                    for c in range(2):
                        r = mm(o_all[:, g, :], c_pT[:, g, c, :], c_v[par][:, c, g * J * HD:(g + 1) * J * HD],
                               start=(c == 0), stop=(c == 1))
                r.then_inc(c_o, 1)
                more = not (last and u >= 2)
                if more:
                    pe.wait_ge(ctx_in[par], 16 * (SPT // 2 * i + (u + 2) // 2 + 1))
                    c_keys(par)
                pe.wait_ge(c_omd, n + 1)
                pe.wait_ge(c_otc, 1 + n)
                for half in range(KI):
                    r = mm(ob[:, D + half * L:D + (half + 1) * L], c_om[:, 2 * half:2 * half + 2, :], sel[:],
                           start=True, stop=True)
                r.then_inc(c_ot, 1)
                if not (last and u == SPT - 1):
                    pe.wait_ge(v_copied, n + 2)
                if u == SPT - 1:
                    pe.wait_ge(c_otc, 1 + n + 1)
                    project_rows(vb[:, 0:D], c_oT, x1_wo).then_inc(c_y, 1)
                if more:
                    if u == SPT - 1:
                        pe.wait_ge(c_x, i + 1)
                    c_values(par)

            for l in range(NL):
                pe.wait_ge(q_all, 1 + tile(NT - 1, l))
            pe.wait_ge(c_kl_done, 1)
            pe.wait_ge(c_vl_done, 1)
            pe.wait_ge(ctx_in[0], 16)
            c_keys(0)
            c_values(0)
            pe.wait_ge(k_copied, 1)
            pe.wait_ge(klast_copied, 1)
            pe.wait_ge(c_q, 1)
            c_scores(0)
            pe.wait_ge(ctx_in[1], 16)
            c_keys(1)
            pe.wait_ge(v_copied, 1)
            c_values(1)
            with pe.Fori(0, T - 1) as i:
                for u in range(SPT):
                    c_step(i, u, False)
            for u in range(SPT):
                c_step(T - 1, u, True)

            pe.wait_ge(c_x, T)
            run_lanes(pe, SLOTS1, [
                attention(A1, "a1", [(2, p_turn), (4, p_project), (8, p_slots), (11, p_scores), (15, p_turn_probs),
                                     (17, p_values), (19, p_gather), (21, p_out)])])

            for l in range(NL):
                pe.wait_ge(s["x_updated"], tile(3 * NT - 1, l))
            pe.wait_ge(in_w["ffn"], 16 * 3)

            def g_turn(b):
                pe.wait_ge(g_xn, b + 1)
                for ki in range(KI):
                    for t in range(TPB):
                        r = tr(ps[:, 6 + ki, t * P:(t + 1) * P], f_xn[:, t, ki * P:(ki + 1) * P], ident[:])
                    r.then_inc(g_xT, 1)

            def g_block(b, last):
                pe.wait_ge(g_xTc, 2 * b + 2)
                for o in range(NF1):
                    if o >= 2:
                        pe.wait_ge(g_h, NF1 * b + o - 1)
                    else:
                        pe.wait_ge(g_ge2, 1 + NF1 * b)
                        pe.wait_ge(g_ys, 1 + TPB * b)
                    project(ps[:, o % 2, :], f_w1, f_xnT, o)
                    project(ps[:, 2 + o % 2, :], f_w2, f_xnT, o).then_inc(g_ab, 1)
                for h, (w, src, done, prev, read, ring) in enumerate((
                        (f_h1, f_ha, g_h1, g_h, g_ge1, RING1), (f_h2, f_hb, g_h2, g_ge1, g_ge2, RING2))):
                    for o in range(NF1):
                        if o >= 4:
                            pe.wait_ge(read, h + NF1 * b + o - 3)
                        for k in range(NF1):
                            if o == 0:
                                pe.wait_ge(prev, NF1 * b + k + 1)
                            r = mm(ps[:, ring[o % 4], :], w[:, k, o * P:(o + 1) * P], src[:, k, :],
                                   start=(k == 0), stop=(k == NF1 - 1))
                        r.then_inc(done, 1)
                    if h == 0:
                        pe.wait_ge(in_w["ffn2"], 16 * 2)
                        if not last:
                            g_turn(b + 1)
                for t in range(TPB):
                    if t >= 2:
                        pe.wait_ge(g_ys, 1 + TPB * b + t - 1)
                    else:
                        pe.wait_ge(g_ys, 1 + TPB * b)
                    for k in range(NF1):
                        if t == 0:
                            pe.wait_ge(g_ge2, 1 + NF1 * b + k + 1)
                        r = mm(ps[:, RING3[t % 2], 0:D], f_ha[:, k, t * P:(t + 1) * P], f_w3[:, k, :],
                               start=(k == 0), stop=(k == NF1 - 1))
                    r.then_inc(g_w3, 1)

            g_turn(0)
            with pe.Fori(0, NB - 1) as b:
                g_block(b, False)
            g_block(NB - 1, True)

        @block.scalar
        def _(act):
            for m in free["act"]:
                act.sem_inc(m, 1)
            af = nc.scalar.activation

            def a_xnT(kind, l, n):
                act.wait_ge(s["xnT_ready"], tile(n, l))
                af(xnT[l], halves(bank[l][0])[:, 0:KI, :], ACT.Copy).then_inc(s["xnT_copied"], 1)

            def a_keys(kind, l, n):
                if kind == A1:
                    act.wait_ge(s["qk_slots_ready"], tile(n - BASE[A1], l))
                    af(kT[l], bank[l][1], ACT.Copy).then_inc(s["k_copied"], 1)
                    return
                act.wait_ge(s["qk_ready"], tile(n, l))
                for fo in range(KI):
                    r = af(qT[l][:, fo * P:(fo + 1) * P], bank[l][0][:, fo * P:(fo + 1) * P],
                           ACT.Identity, bias=colb[:, BIAS_Q[kind], fo:fo + 1])
                r.then_inc(s["q_copied"], 1)
                for fo in range(KI):
                    r = af(kT[l][:, fo * P:(fo + 1) * P], bank[l][0][:, (KI + fo) * P:(KI + fo + 1) * P],
                           ACT.Identity, bias=colb[:, BIAS_K[kind], fo:fo + 1])
                r.then_inc(s["k_copied"], 1)

            def a_spread(kind, l, n):
                act.wait_ge(s["v_ready"], tile(n, l))
                for b in range(SPT):
                    rows = slice(b * L, (b + 1) * L)
                    r = af(vbd[l][rows, b, :], bank[l][1][rows, 0:D], ACT.Copy)
                r.then_inc(s["v_spread"], 1)

            def a_lines(kind, l, n):
                act.wait_ge(s["v_ready"], tile(n, l))
                af(pp[l][:, :, :, :], bank[l][1][:, D:D + 8 * H].rearrange("p (a h c) -> p a h c", a=2, c=4),
                   ACT.Copy).then_inc(s["lines_in"], 1)

            def a_gate(kind, l, n):
                act.wait_ge(s["v_ready"], tile(n, l))
                for fo in range(KI):
                    r = af(gT[l][:, fo, :], halves(bank[l][1])[:, KI + fo, :], ACT.Exp, scale=-1.0,
                           bias=nbg[:, fo:fo + 1])
                r.then_inc(s["gate_exp"], 1)

            def a_exp(kind, l, n):
                act.wait_ge(s["scores_shifted"], tile(n, l))
                af(pr[l].rearrange("p g (b k) -> p (g b) k", k=L), sc[l], ACT.Exp).then_inc(s["probs_ready"], 1)

            def a_pT(kind, l, n):
                act.wait_ge(s["pT_ready"], tile(n, l))
                af(pT[l], bank[l][1].rearrange("p (g t) -> p g t", t=P), ACT.Copy).then_inc(s["pT_copied"], 1)

            act.wait_ge(in_const, 16 * N_CONST)
            act.wait_ge(gate_bias_ready, 1)
            act.wait_ge(consts_made, 1)

            def attention(kind, steps):
                return (lambda: None,
                        [(at, lambda l, i, step=step: step(kind, l, i + (NORM if step is a_xnT else BASE)[kind]))
                         for at, step in steps])

            run_lanes(act, SLOTS0, [
                attention(X0, [(3, a_xnT), (5, a_keys), (5, a_spread), (9, a_exp), (11, a_pT)]),
                attention(A0, [(2, a_xnT), (4, a_keys), (4, a_spread), (4, a_gate), (7, a_exp), (9, a_pT)])])

            for m in range(3):
                for c in range(3):
                    act.wait_ge(wT_turned, 3 * m + c + 1)
                    at = WT + 1536 * m + 512 * c
                    af(view(at, 512), ps[:, (3 * m + c) % 8, :], ACT.Copy).then_inc(wT_copied, 1)
            ugb = ug.rearrange("p f (b t) -> p f b t", t=BLK)
            with act.Fori(0, NB // 2) as i:
                for u in range(2):
                    b = 2 * i + u
                    for ki in range(KI):
                        act.wait_ge(f0_xT, 1 + 2 * b + ki + 1)
                        act.wait_ge(f0_ug, 1 + 2 * NF0 * b)
                        af(xqT[u][:, ki, :], ps[:, 6 + ki, :], ACT.Copy).then_inc(f0_xTc, 1)
                    for f in range(2 * NF0):
                        act.wait_ge(f0_ug, 1 + 2 * NF0 * b + f + 1)
                        stand(act, "act")
                        af(ugb[:, f, b, :], ps[:, f % 4, :], ACT.Copy).then_inc(f0_ugc, 1)
            act.wait_ge(f0_scale, 2)
            for f in range(NF0):
                af(ug[:, f + NF0, :], ug[:, f + NF0, :], ACT.Identity, scale=qinv[:, QG:QG + 1],
                   bias=magic[:, :]).then_inc(f0_gr, 1)
            for j in range(0, NF0, 2):
                for f in (j, j + 1):
                    act.wait_ge(f0_gq, f + 1)
                    if f >= 4:
                        act.wait_ge(f0_g2, 1 + f - 3)
                    af(sg[f % 4], ug[:, f + NF0, :], ACT.Sigmoid).then_inc(f0_sg, 1)
                for f in (j, j + 1):
                    act.wait_ge(f0_sg, f + 1)
                    af(sg[f % 4], sg[f % 4], ACT.Identity, scale=65536.0, bias=magic[:, :]).then_inc(f0_sgr, 1)
                act.wait_ge(f0_sgr, j + 1)
                af(sg[j % 4], sg[j % 4], ACT.Identity, scale=1.0 / 65536.0, bias=unmagic[:, :]).then_inc(f0_sr_act, 1)
            act.wait_ge(f0_scale, 3)
            with act.Fori(0, NF0) as f:
                af(ug[:, f + NF0, :], ug[:, f + NF0, :], ACT.Identity, scale=qinv[:, QS:QS + 1],
                   bias=magic[:, :]).then_inc(f0_g2r, 1)
            act.wait_ge(f0_scale, 4)
            with act.Fori(0, NB // 2) as i:
                for u in range(2):
                    b = 2 * i + u
                    act.wait_ge(f0_y, 1 + TPB * 2 * i)
                    stand(act, "act")
                    for f in range(NF0):
                        af(oq[u][:, f, :], ugb[:, f, b, :], ACT.Identity, scale=qinv[:, QO:QO + 1],
                           bias=magic[:, :]).then_inc(f0_or, 1)

            act.wait_ge(c_kl_ps, 1)
            act.wait_ge(f0_x, 1 + T)
            for fo in range(KI):
                r = af(c_klast[:, fo, :], ps[:, 2, fo * NSEQ:(fo + 1) * NSEQ], ACT.Identity,
                       bias=colb[:, BK1, fo:fo + 1])
            r.then_inc(c_kl_done, 1)
            with act.Fori(0, NT) as i:
                for l in range(NL):
                    a_xnT(None, l, i + 2 * NT)

            def c_keys(par, count):
                act.wait_ge(k_ready, count)
                for fo in range(KI):
                    r = af(c_kT[par][:, fo, 0:2 * P], ps[:, 4, fo * D:(fo + 1) * D], ACT.Identity,
                           bias=colb[:, BK1, fo:fo + 1])
                r.then_inc(k_copied, 1)

            def c_values(par, count):
                act.wait_ge(v_ready, count)
                af(c_v[par].rearrange("p c e -> p (c e)"), ps[:, 5, :], ACT.Copy).then_inc(v_copied, 1)

            def c_exps(par, n):
                for g in range(G):
                    act.wait_ge(c_max, G * n + g + 1)
                    af(c_p[:, g, :], ps[:, g, 0:S], ACT.Exp, bias=c_nmx[par][:, g:g + 1],
                       accum_out=c_sum[par][:, g:g + 1]).then_inc(c_exp, 1)

            def c_step(i, u, last):
                n = SPT * i + u
                if not (last and u == SPT - 1):
                    act.wait_ge(c_rinv, 1 + n)
                    act.wait_ge(c_lastk, 1 + n + 1)
                    c_exps((u + 1) % 2, n + 1)
                if not (last and u >= 2):
                    c_keys(u % 2, n + 3)
                    c_values(u % 2, n + 3)

            for l in range(NL):
                act.wait_ge(q_all, 1 + tile(NT - 1, l))
            c_keys(0, 1)
            c_values(0, 1)
            c_exps(0, 0)
            c_keys(1, 2)
            c_values(1, 2)
            with act.Fori(0, T - 1) as i:
                for u in range(SPT):
                    c_step(i, u, False)
            for u in range(SPT):
                c_step(T - 1, u, True)
            act.wait_ge(c_x, T)
            act.wait_ge(consts_made, 2)
            run_lanes(act, SLOTS1, [
                attention(A1, [(3, a_xnT), (4, a_lines), (4, a_spread), (9, a_keys), (14, a_exp), (16, a_pT)])])

            for l in range(NL):
                act.wait_ge(s["x_updated"], tile(3 * NT - 1, l))

            def g_turned(b):
                for ki in range(KI):
                    act.wait_ge(g_xT, 1 + 2 * b + ki + 1)
                    af(f_xnT[:, ki, :], ps[:, 6 + ki, :], ACT.Copy).then_inc(g_xTc, 1)

            def g_block(b, last):
                for o in range(NF1):
                    act.wait_ge(g_ab, NF1 * b + o + 1)
                    if o >= 2:
                        act.wait_ge(g_h, NF1 * b + o - 1)
                    af(f_silu[:, o % 2, :], ps[:, o % 2, :], ACT.Silu, scale=ffn_s[:, 0, o:o + 1]).then_inc(g_sil, 1)
                for o in range(NF1):
                    act.wait_ge(g_h1, NF1 * b + o + 1)
                    af(f_hb[:, o, :], ps[:, RING1[o % 4], :], ACT.Gelu, scale=ffn_s[:, 2, o:o + 1]).then_inc(g_ge1, 1)
                if not last:
                    g_turned(b + 1)
                for o in range(NF1):
                    act.wait_ge(g_h2, NF1 * b + o + 1)
                    af(f_ha[:, o, :], ps[:, RING2[o % 4], :], ACT.Gelu, scale=ffn_s[:, 3, o:o + 1]).then_inc(g_ge2, 1)

            g_turned(0)
            with act.Fori(0, NB - 1) as b:
                g_block(b, False)
            g_block(NB - 1, True)

        @block.vector
        def _(dve):
            for m in free["dve"]:
                dve.sem_inc(m, 1)
            v = nc.vector

            def d_norm(kind, l, i, n):
                if kind == A0:
                    dve.wait_ge(s["x_updated"], tile(i, l))
                    stand(dve, "dve")
                v.bn_stats(stats[l][:, :], xl[:, i, l, :]).then_inc(s["stats_ready"], 1)
                dve.wait_ge(s["stats_ready"], tile(n, l))
                stand(dve, "dve")
                v.bn_aggr(mv[l][:, :], stats[l][:, :]).then_inc(s["mv_ready"], 1)

            def d_scale(kind, l, i, n):
                dve.wait_ge(s["rstd_ready"], tile(n, l))
                v.tensor_scalar(xn[l], xl[:, i, l, :], mv[l][:, 0:1], rstd[l][:, :], ALU.subtract, ALU.mult)\
                    .then_inc(s["xn_ready"], 1)

            def d_queries(kind, l, i, n):
                if kind == A1:
                    dve.wait_ge(s["qk_slots_ready"], tile(n - BASE[A1], l))
                    q = bank[l][0].rearrange("p (c q) -> p c q", q=L).unsqueeze(2).broadcast_to([P, H, J, L])
                    m = mask4[:, :].unsqueeze(1).unsqueeze(3).broadcast_to([P, H, J, L])
                    v.tensor_tensor(qbd[l].rearrange("p (c j q) -> p c j q", j=J, q=L), q, m, ALU.mult)\
                        .then_inc(s["q_masked"], 1)
                    return
                dve.wait_ge(s["q_copied"], tile(n, l))
                q = qT[l].rearrange("p (c q) -> p c q", q=L).unsqueeze(2).broadcast_to([P, 8, 8, L])
                m = mask8[:, :].unsqueeze(1).unsqueeze(3).broadcast_to([P, 8, 8, L])
                v.tensor_tensor(qbd[l].rearrange("p (c h q) -> p c h q", h=8, q=L), q, m, ALU.mult)\
                    .then_inc(s["q_masked"], 1)

            def d_slots(kind, l, i, n):
                m = n - BASE[A1]
                dve.wait_ge(s["qk_ready"], tile(n, l))
                for d, c, done in ((qs[l], 0, "q_evac"), (ks[l], 1, "k_slots")):
                    src = bank[l][0][:, c * D:(c + 1) * D].rearrange("p (h e) -> p h e", e=HD)
                    b = a1_bqk[:, c * D:(c + 1) * D].rearrange("p (h e) -> p h e", e=HD)
                    r = v.tensor_tensor(d[:, :, 0:HD], src, b, ALU.add)
                    if c == 1:
                        r.then_inc(s["q_evac"], 1)

            def d_lines(kind, l, i, n):
                m = n - BASE[A1]
                dve.wait_ge(s["lines_sq"], tile(m, l))
                v.tensor_reduce(lsq[l][:, :], lb[l][:, :, :], AX.X, ALU.add).then_inc(s["lines_sum"], 1)
                dve.wait_ge(s["lines_sum"], 2 * (NL * m + l) + 1)
                v.tensor_scalar(lsq[l][:, :], lsq[l][:, :], 1e-24, None, ALU.max).then_inc(s["lines_sum"], 1)

            def d_mask(kind, l, i, n):
                dve.wait_ge(s["scores_ready"], tile(n, l))
                mk = posmask if kind == A0 else causal
                v.scalar_tensor_tensor(sc[l].rearrange("p c k -> p (c k)"), bank[l][0], 0.25, mk[:, :],
                                       ALU.mult, ALU.add).then_inc(s["scores_masked"], 1)

            def d_max(kind, l, i, n):
                dve.wait_ge(s["scores_masked"], tile(n, l))
                v.tensor_reduce(nmx[l][:, :], sc[l], AX.X, ALU.max, negate=True).then_inc(s["max_ready"], 1)

            def d_shift(kind, l, i, n):
                dve.wait_ge(s["max_ready"], tile(n, l))
                v.tensor_tensor(sc[l], sc[l], nmx[l][:, :].unsqueeze(2).broadcast_to([P, H, L]), ALU.add)\
                    .then_inc(s["scores_shifted"], 1)

            def d_sums(kind, l, i, n):
                dve.wait_ge(s["probs_ready"], tile(n, l))
                v.tensor_reduce(rsum[l][:, :], pr[l].rearrange("p g (b k) -> p (g b) k", k=L), AX.X, ALU.add)\
                    .then_inc(s["sum_ready"], 1)
                dve.wait_ge(s["sum_ready"], 3 * (NL * n + l) + 1)
                v.reciprocal(rinv[l][:, :].rearrange("p (a b g) -> p a g b", a=KI, g=2),
                             rsum[l][:, :].rearrange("p (a g b) -> p a g b", a=KI, g=2)).then_inc(s["sum_ready"], 1)
                dve.wait_ge(s["sum_ready"], 3 * (NL * n + l) + 2)
                v.tensor_tensor(rm[l][:, :, :], rinv[l][:, :].unsqueeze(2).broadcast_to([P, H, J]),
                                mask4[:, :].unsqueeze(1).broadcast_to([P, H, J]), ALU.mult)\
                    .then_inc(s["sum_ready"], 1)

            def d_gate1(kind, l, i, n):
                m = n - BASE[A0]
                dve.wait_ge(s["gate_exp"], tile(m, l))
                v.tensor_scalar(gT[l], gT[l], 1.0, None, ALU.add).then_inc(s["gate_plus"], 1)

            def d_gate2(kind, l, i, n):
                m = n - BASE[A0]
                dve.wait_ge(s["gate_plus"], tile(m, l))
                v.reciprocal(gT[l], gT[l]).then_inc(s["gate_done"], 1)

            def d_own(kind, l, i, n):
                dve.wait_ge(s["sum_ready"], 3 * (NL * n + l) + 3)
                dve.wait_ge(s["o_ready"], tile(n, l))
                o = ps[:, 2 * l:2 * l + 2, :].rearrange("p k (c j e) -> p (k c) j e", j=J, e=HD)
                v.tensor_tensor(om[l].rearrange("p (c j e) -> p c j e", j=J, e=HD), o,
                                rm[l][:, :, :].unsqueeze(3).broadcast_to([P, H, J, HD]), ALU.mult)\
                    .then_inc(s["o_normed"], 1)

            def d_oT(kind, l, i, n):
                dve.wait_ge(s["oT_ready"], tile(n, l))
                src = bank[l][0][:, D:2 * D].rearrange("p (a t) -> p a t", t=P)
                if kind == A0:
                    dve.wait_ge(s["gate_done"], tile(n - BASE[A0], l))
                    for fo in range(KI):
                        r = v.scalar_tensor_tensor(oT[l][:, fo, :], src[:, fo, :], colb[:, BVA, fo:fo + 1],
                                                   gT[l][:, fo, :], ALU.add, ALU.mult)
                else:
                    r = v.tensor_tensor(oT[l], src, BIAS_V[kind].unsqueeze(2).broadcast_to([P, KI, P]), ALU.add)
                r.then_inc(s["oT_copied"], 1)

            def d_add(kind, l, i, n):
                dve.wait_ge(s["y_ready"], tile(n, l))
                dve.wait_ge(s["x_biased"], tile(n - BASE[kind] + NORM[kind], l))
                v.tensor_tensor(xl[:, i, l, :], xl[:, i, l, :], bank[l][1][:, 0:D], ALU.add)\
                    .then_inc(s["x_updated"], 1)

            def w_part(m, i):
                return [a.rearrange("p (i b) c -> p i b c", i=NT)[:, i] for a in
                        (w_nat[m], wmax[:, m], wsc[:, m], winv[:, m])]

            def d_w_max(kind, m, i, n):
                if m < 3:
                    w, wm, ws, wi = w_part(m, i)
                    v.tensor_reduce(wm, w, AX.X, ALU.max, apply_absolute_value=True).then_inc(w_max, 1)

            def d_w_scale(kind, m, i, n):
                if m < 3:
                    w, wm, ws, wi = w_part(m, i)
                    dve.wait_ge(w_max, 3 * i + m + 1)
                    v.tensor_scalar(ws, wm, 1.0 / 7.0, 1e-12, ALU.mult, ALU.max).then_inc(w_scale, 1)

            def d_w_inverse(kind, m, i, n):
                if m < 3:
                    w, wm, ws, wi = w_part(m, i)
                    dve.wait_ge(w_scale, 3 * i + m + 1)
                    v.reciprocal(wi, ws).then_inc(w_inverse, 1)

            def d_w_divide(kind, m, i, n):
                if m < 3:
                    w, wm, ws, wi = w_part(m, i)
                    dve.wait_ge(w_inverse, 3 * i + m + 1)
                    v.tensor_tensor(w, w, wi.broadcast_to(W_PART), ALU.mult).then_inc(w_divided, 1)

            def d_w_round(kind, m, i, n):
                if m < 3:
                    w, wm, ws, wi = w_part(m, i)
                    dve.wait_ge(w_divided, 3 * i + m + 1)
                    v.tensor_scalar(w, w, MAGIC, None, ALU.add).then_inc(w_rounded, 1)

            def d_w_multiply(kind, m, i, n):
                if m < 3:
                    w, wm, ws, wi = w_part(m, i)
                    dve.wait_ge(w_rounded, 3 * i + m + 1)
                    v.scalar_tensor_tensor(w, w, -MAGIC, ws.broadcast_to(W_PART), ALU.add, ALU.mult)\
                        .then_inc(wT_quant, 1)

            def d_f_stats(kind, l, i, n):
                dve.wait_ge(s["x_updated"], tile(n, l))
                v.bn_stats(f_stats4[:, i, l, :], xl[:, i, l, :]).then_inc(f0_stats, 1)

            def attention(kind, steps, enter=lambda: None):
                return (enter, [(at, lambda l, i, step=step: step(
                    kind, l, i, i + (NORM if step in (d_norm, d_scale) else BASE)[kind])) for at, step in steps])

            v.memset(magic[:, :], MAGIC)
            v.memset(unmagic[:, :], -MAGIC / 65536.0)
            for l in range(NL):
                v.memset(vbd[l], 0.0)
            v.memset(minus_half[:, :], -0.5).then_inc(consts_made, 1)
            dve.wait_ge(in_const, 16 * N_CONST)
            v.tensor_scalar(nbg[:, :], colb[:, BG, :], -1.0, None, ALU.mult).then_inc(gate_bias_ready, 1)
            dve.wait_ge(in_x, 32)

            def enter_a0():
                dve.wait_ge(in_later_const, 16 * N_LATER_CONST)
                v.tensor_tensor(posmask[:, :], posmask[:, :], causal[:, :], ALU.add).then_inc(posmask_ready, 1)
                v.tensor_scalar(plscale[:, :], plscale[:, :], 4.0, None, ALU.mult).then_inc(pl_scale_ready, 1)
                dve.wait_ge(pl_scale_ready, 1)
                v.tensor_tensor(plsc[:, :, :], plscale[:, :].unsqueeze(2).broadcast_to([P, H, NLINE]),
                                plsign[:, :].unsqueeze(1).broadcast_to([P, H, NLINE]), ALU.mult)\
                    .then_inc(pl_scale_ready, 1)
                dve.wait_ge(posmask_ready, 1)
                dve.wait_ge(in_w["nat"], 48)

            run_lanes(dve, SLOTS0, [
                attention(X0, [(0, d_norm), (1, d_scale), (6, d_queries), (8, d_mask), (8, d_max), (8, d_shift),
                               (10, d_sums), (13, d_own), (15, d_oT), (17, d_add)]),
                attention(A0, [(0, d_norm), (1, d_scale), (4, d_queries), (5, d_gate1), (6, d_mask), (6, d_max),
                               (6, d_shift), (8, d_sums), (9, d_gate2), (11, d_own), (13, d_oT), (15, d_add),
                               (2, d_w_max), (3, d_w_scale), (4, d_w_inverse), (7, d_w_divide), (10, d_w_round),
                               (12, d_w_multiply), (16, d_f_stats)], enter_a0)])

            def scales(i0, i1, done):
                dve.wait_ge(f0_allmax, done)
                link(dve, dve_link, v.tensor_scalar(qsc[:, i0:i1], allmax[:, i0:i1], 1.0 / QMAX, 1e-12,
                                                    ALU.mult, ALU.max))
                v.reciprocal(qinv[:, i0:i1], qsc[:, i0:i1]).then_inc(f0_scale, 1)
                dve.wait_ge(f0_scale, done)

            def quantized(o, i, k):
                return v.tensor_scalar(o, i, -MAGIC, qsc[:, k:k + 1], ALU.add, ALU.mult)

            dve.wait_ge(f0_stats, T)
            for t in range(T):
                v.bn_aggr(f_mv[:, t, :], f_stats[:, t, :]).then_inc(f0_mv, 1)
            dve.wait_ge(f0_rstd, 1)
            dve.wait_ge(wT_turned, 9)
            for t in range(T):
                r = v.tensor_scalar(xall[:, t, :], x[:, t, :], f_mv[:, t, 0:1], f_rstd[:, t:t + 1],
                                    ALU.subtract, ALU.mult)
            link(dve, dve_link, r)
            v.tensor_reduce(pmax[:, QX:QX + 1], xall, AX.XY, ALU.max, apply_absolute_value=True).then_inc(f0_pmax, 1)
            scales(QX, QX + 1, 1)
            link(dve, dve_link, v.tensor_scalar(xall, xall, qinv[:, QX:QX + 1], MAGIC, ALU.mult, ALU.add))
            xab = xall.rearrange("p (b t) d -> p b t d", t=TPB)
            with dve.Fori(0, NB // 2) as i:
                for u in range(2):
                    b = 2 * i + u
                    dve.wait_ge(f0_xT, 1 + 2 * 2 * i)
                    quantized(xq[u], xab[:, b, :, :], QX).then_inc(f0_xq, 1)
                    for f in range(2 * NF0):
                        dve.wait_ge(f0_ugc, 1 + 2 * NF0 * b + f + 1)
                        v.tensor_reduce(amax[:, f, b, :], ug.rearrange("p f (b t) -> p f b t", t=BLK)[:, f, b, :], AX.X, ALU.max,
                                        apply_absolute_value=True).then_inc(f0_ugm, 1)
            dve.wait_ge(f0_ugm, 2 * NF0 * NB)
            v.tensor_reduce(pmax[:, QU:QG + 1], amax[:, :, :, :].rearrange("p (a f) b c -> p a (f b c)", a=2), AX.X, ALU.max)\
                .then_inc(f0_pmax, 1)
            scales(QU, QG + 1, 2)
            for f in range(NF0):
                g = ug[:, f + NF0, :]
                dve.wait_ge(f0_gr, f + 1)
                quantized(g, g, QG).then_inc(f0_gq, 1)
            for f in range(NF0):
                g = ug[:, f + NF0, :]
                dve.wait_ge(f0_gq, f + 1)
                dve.wait_ge(f0_sr_pool if f % 2 else f0_sr_act, f // 2 + 1)
                v.scalar_tensor_tensor(g, sg[f % 4], 65535.0 / 65536.0, g, ALU.min, ALU.mult).then_inc(f0_g2, 1)
                dve.wait_ge(f0_g2, 1 + f + 1)
                v.tensor_reduce(amax[:, f, 0, :], g, AX.X, ALU.max, apply_absolute_value=True).then_inc(f0_ugm, 1)
            dve.wait_ge(f0_ugm, 2 * NF0 * NB + NF0)
            v.tensor_reduce(pmax[:, QS:QS + 1], amax[:, 0:NF0, 0, 0], AX.X, ALU.max).then_inc(f0_pmax, 1)
            scales(QS, QS + 1, 3)
            dve.wait_ge(f0_uq, NF0 // 2)
            with dve.Fori(0, NF0) as f:
                g, up = ug[:, f + NF0, :], ug[:, f, :]
                dve.wait_ge(f0_g2r, f + 1)
                v.scalar_tensor_tensor(up, g, -MAGIC, up, ALU.add, ALU.mult).then_inc(f0_o, 1)
                dve.wait_ge(f0_o, f + 1)
                v.tensor_reduce(amax[:, f, 1, :], up, AX.X, ALU.max, apply_absolute_value=True).then_inc(f0_ugm, 1)
            dve.wait_ge(f0_ugm, 2 * NF0 * NB + 2 * NF0)
            v.tensor_reduce(pmax[:, QO:QO + 1], amax[:, 0:NF0, 1, 0], AX.X, ALU.max).then_inc(f0_pmax, 1)
            dve.wait_ge(f0_allmax, 4)
            link(dve, dve_link, v.tensor_tensor(allmax[:, QO:QO + 1], allmax[:, QO:QO + 1], qsc[:, QS:QS + 1], ALU.mult))
            link(dve, dve_link, v.tensor_scalar(qsc[:, QO:QO + 1], allmax[:, QO:QO + 1], 1.0 / QMAX, 1e-12,
                                                ALU.mult, ALU.max))
            link(dve, dve_link, v.reciprocal(qinv[:, QO:QO + 1], qsc[:, QO:QO + 1]))
            v.tensor_tensor(qinv[:, QO:QO + 1], qinv[:, QO:QO + 1], qsc[:, QS:QS + 1], ALU.mult).then_inc(f0_scale, 1)
            with dve.Fori(0, NB // 2) as i:
                for u in range(2):
                    b = 2 * i + u
                    for f in range(NF0):
                        dve.wait_ge(f0_or, NF0 * b + f + 1)
                        quantized(oq[u][:, f, :], oq[u][:, f, :], QO).then_inc(f0_oq, 1)
                    for t in range(TPB):
                        dve.wait_ge(f0_y, 1 + TPB * b + t + 1)
                        xt = x[:, :, :].rearrange("p (b t) d -> p b t d", t=TPB)[:, b, t, :]
                        v.tensor_tensor(xt, xt, ps[:, 4 * u + t, 0:D], ALU.add).then_inc(f0_x, 1)
            dve.wait_ge(f0_x, 1 + T)

            dve.wait_ge(c_vl_ps, 1)
            v.tensor_copy(c_vlast[0:NSEQ, :], ps[0:NSEQ, 3, 0:D]).then_inc(c_vl_done, 1)
            q_lane = qT_all.rearrange("p a (i l t) -> p a i l t", l=NL, t=P)
            with dve.Fori(0, NT) as i:
                for l in range(NL):
                    d_norm(None, l, i, i + 2 * NT)
                for l in range(NL):
                    d_scale(None, l, i, i + 2 * NT)
                for l in range(NL):
                    dve.wait_ge(s["q_evac"], tile(i, l))
                    for fo in range(KI):
                        r = v.tensor_scalar(q_lane[:, fo, i, l, :], bank[l][1][:, fo * P:(fo + 1) * P],
                                            colb[:, BQ1, fo:fo + 1], 0.25, ALU.add, ALU.mult)
                    r.then_inc(q_all, 1)

            def c_maxes(par, n):
                for g in range(G):
                    dve.wait_ge(c_s, G * n + g + 1)
                    v.tensor_reduce(c_nmx[par][:, g:g + 1], ps[:, g, 0:S], AX.X, ALU.max, negate=True)\
                        .then_inc(c_max, 1)

            def c_step(i, u, last):
                n = SPT * i + u
                dve.wait_ge(c_o, 1 + n)
                for k, bk in ((0, 6), (1, 4)):
                    dve.wait_ge(c_pt, 2 * n + k + 1)
                    v.tensor_copy(c_pT[:, 2 * k:2 * k + 2, :, :].rearrange("p g c t -> p (g c t)"), ps[:, bk, :])\
                        .then_inc(c_ptc, 1)
                dve.wait_ge(c_exp, 4 * n + 4)
                v.reciprocal(c_inv[:, :], c_sum[u % 2][:, :]).then_inc(c_rinv, 1)
                if not (last and u == SPT - 1):
                    c_maxes((u + 1) % 2, n + 1)
                dve.wait_ge(c_rinv, 1 + n + 1)
                v.tensor_tensor(c_rm[:, :, :], c_inv[:, :].unsqueeze(2).broadcast_to([P, G, J]),
                                mask4[:, :].unsqueeze(1).broadcast_to([P, G, J]), ALU.mult).then_inc(c_rmd, 1)
                dve.wait_ge(c_rmd, n + 1)
                dve.wait_ge(c_o, 1 + n + 1)
                dve.wait_ge(c_lastk, 1 + n + 1)
                v.tensor_tensor(c_osum, c_osum, ps[:, 7, 0:D].rearrange("p (g e) -> p g e", g=G), ALU.add)\
                    .then_inc(c_added, 1)
                dve.wait_ge(c_added, n + 1)
                dve.wait_ge(c_ot, 1 + n)
                v.tensor_tensor(c_om.rearrange("p g (j e) -> p g j e", e=HD),
                                c_osum.rearrange("p g (j e) -> p g j e", e=HD),
                                c_rm[:, :, :].unsqueeze(3).broadcast_to([P, G, J, HD]), ALU.mult).then_inc(c_omd, 1)
                dve.wait_ge(c_ot, 1 + n + 1)
                if u == 0:
                    dve.wait_ge(c_y, 1 + i)
                v.tensor_tensor(c_oT[:, :, u * L:(u + 1) * L],
                                ps[:, 7, D:D + KI * L].rearrange("p (a q) -> p a q", q=L),
                                colb[:, BV1, :].unsqueeze(2).broadcast_to([P, KI, L]), ALU.add).then_inc(c_otc, 1)
                if u == SPT - 1:
                    dve.wait_ge(c_y, 1 + i + 1)
                    v.tensor_tensor(x[:, i, :], x[:, i, :], ps[:, 5, 0:D], ALU.add).then_inc(c_x, 1)

            for l in range(NL):
                dve.wait_ge(q_all, 1 + tile(NT - 1, l))
                dve.wait_ge(s["x_biased"], tile(3 * NT - 1, l))
            c_maxes(0, 0)
            with dve.Fori(0, T - 1) as i:
                for u in range(SPT):
                    c_step(i, u, False)
            for u in range(SPT):
                c_step(T - 1, u, True)
            dve.wait_ge(c_x, T)
            for l in range(NL):
                v.memset(vbd[l], 0.0)
                v.memset(qs[l], 0.0)
                r = v.memset(ks[l], 0.0)
            r.then_inc(consts_made, 1)
            dve.wait_ge(consts_made, 2)
            run_lanes(dve, SLOTS1, [
                attention(A1, [(0, d_norm), (1, d_scale), (4, d_slots), (5, d_lines), (9, d_queries), (13, d_mask),
                               (13, d_max), (13, d_shift), (15, d_sums), (19, d_own), (20, d_oT), (22, d_add)])])
            for l in range(NL):
                dve.wait_ge(s["x_updated"], tile(3 * NT - 1, l))

            xb = x[:, :, :].rearrange("p (b t) d -> p b t d", t=TPB)

            def g_norm(b):
                for t in range(TPB):
                    v.bn_stats(g_stats[:, t, :], xb[:, b, t, :]).then_inc(g_st, 1)
                dve.wait_ge(g_st, TPB * b + TPB)
                stand(dve, "dve")
                for t in range(TPB):
                    v.bn_aggr(g_mv[:, t, :], g_stats[:, t, :]).then_inc(g_mvd, 1)
                dve.wait_ge(g_rs, b + 1)
                dve.wait_ge(g_xT, 1 + 2 * b)
                for t in range(TPB):
                    r = v.tensor_scalar(f_xn[:, t, :], xb[:, b, t, :], g_mv[:, t, 0:1], g_rstd[:, t:t + 1],
                                        ALU.subtract, ALU.mult)
                r.then_inc(g_xn, 1)

            def g_block(b, last):
                for o in range(NF1):
                    dve.wait_ge(g_sil, NF1 * b + o + 1)
                    v.scalar_tensor_tensor(f_ha[:, o, :], ps[:, 2 + o % 2, :], ffn_s[:, 1, o:o + 1],
                                           f_silu[:, o % 2, :], ALU.mult, ALU.mult).then_inc(g_h, 1)
                if not last:
                    g_norm(b + 1)
                for t in range(TPB):
                    dve.wait_ge(g_w3, TPB * b + t + 1)
                    v.tensor_tensor(f_y[:, t % 2, :], ps[:, RING3[t % 2], 0:D], w3s[:, :], ALU.mult).then_inc(g_ys, 1)
                    dve.wait_ge(g_ys, 1 + TPB * b + t + 1)
                    v.tensor_tensor(xb[:, b, t, :], xb[:, b, t, :], f_y[:, t % 2, :], ALU.add).then_inc(g_x, 1)

            g_norm(0)
            with dve.Fori(0, NB - 1) as b:
                g_block(b, False)
            g_block(NB - 1, True)

        @block.gpsimd
        def _(pool):
            for m in free["pool"]:
                pool.sem_inc(m, 1)
            p = nc.gpsimd

            def rsqrt(l, n):
                pool.wait_ge(s["mv_ready"], tile(n, l))
                stand(pool, "pool")
                p.tensor_scalar(vare[l][:, :], mv[l][:, 1:2], EPS, None, ALU.add).then_inc(s["vare_ready"], 1)
                pool.wait_ge(s["vare_ready"], tile(n, l))
                p.tensor_tensor(rstd[l][:, :], vare[l][:, :], minus_half[:, 0:1],
                                ALU.pow).then_inc(s["rstd_ready"], 1)

            def bias(l, i, n, k):
                pool.wait_ge(s["xn_ready"], tile(n, l))
                p.tensor_tensor(xl[:, i, l, :], xl[:, i, l, :], rowb[:, k, :], ALU.add)\
                    .then_inc(s["x_biased"], 1)

            pool.wait_ge(consts_made, 1)
            pool.wait_ge(in_const, 16 * N_CONST)

            def attention(kind, steps):
                return (lambda: None, [(at, lambda l, i, step=step: step(kind, l, i)) for at, step in steps])

            def b_rsqrt(kind, l, i):
                rsqrt(l, i + NORM[kind])

            def b_bias(kind, l, i):
                bias(l, i, i + NORM[kind], BOUT[kind])

            run_lanes(pool, SLOTS0, [attention(kind, [(0, b_rsqrt), (2, b_bias)]) for kind in (X0, A0)])
            pool.wait_ge(f0_mv, T)
            p.tensor_scalar(f_ve[:, :], f_mv[:, :, 1], EPS, None, ALU.add).then_inc(f0_ve, 1)
            pool.wait_ge(f0_ve, 1)
            p.tensor_tensor(f_rstd[:, :], f_ve[:, :], minus_half[:, 0:T], ALU.pow).then_inc(f0_rstd, 1)
            for k, (i0, i1) in enumerate(((QX, QX + 1), (QU, QG + 1), (QS, QS + 1), (QO, QO + 1))):
                if k == 2:
                    pool.wait_ge(f0_scale, 2)
                    for f in range(0, NF0, 2):
                        up = ug[:, f:f + 2, :]
                        p.tensor_scalar(up, up, qinv[:, QU:QU + 1], MAGIC, ALU.mult, ALU.add).then_inc(f0_ur, 1)
                        pool.wait_ge(f0_ur, f // 2 + 1)
                        p.tensor_scalar(up, up, -MAGIC, qsc[:, QU:QU + 1], ALU.add, ALU.mult).then_inc(f0_uq, 1)
                        pool.wait_ge(f0_sgr, f + 2)
                        p.tensor_scalar(sg[(f + 1) % 4], sg[(f + 1) % 4], -MAGIC, 1.0 / 65536.0, ALU.add, ALU.mult)\
                            .then_inc(f0_sr_pool, 1)
                pool.wait_ge(f0_pmax, k + 1)
                p.partition_all_reduce(allmax[:, i0:i1], pmax[:, i0:i1], P, bass.bass_isa.ReduceOp.max)\
                    .then_inc(f0_allmax, 1)
            pool.wait_ge(f0_x, 1 + T)
            with pool.Fori(0, NT) as i:
                for l in range(NL):
                    rsqrt(l, i + 2 * NT)
                for l in range(NL):
                    bias(l, i, i + 2 * NT, BO1)

            q_seq = qT_all.rearrange("p a (n q) -> p a n q", q=L)

            def c_query(par, n):
                q = q_seq[:, :, n, :].unsqueeze(2).broadcast_to([P, KI, 8, L])
                m = mask8[:, :].unsqueeze(1).unsqueeze(3).broadcast_to([P, KI, 8, L])
                p.tensor_tensor(c_qbd[par], q, m, ALU.mult).then_inc(c_q, 1)
                p.tensor_copy(c_kT[par][:, :, 2 * P:S], klast_seq[:, :, n, :]).then_inc(klast_copied, 1)

            for l in range(NL):
                pool.wait_ge(q_all, 1 + tile(NT - 1, l))
            pool.wait_ge(c_kl_done, 1)
            c_query(0, 0)
            c_query(1, 1)

            def c_step(i, u, last):
                n = SPT * i + u
                pool.wait_ge(c_exp, 4 * n + 4)
                pool.wait_ge(vl_in[u % 2], 16 * (SPT // 2 * i + u // 2 + 1))
                pool.wait_ge(c_ot, 1 + n)
                p.tensor_tensor(c_osum, c_vl[u % 2].rearrange("p (g e) -> p g e", g=G),
                                c_p[:, :, 2 * P:S].broadcast_to([P, G, J * HD]), ALU.mult).then_inc(c_lastk, 1)
                if not (last and u >= 2):
                    pool.wait_ge(c_s, G * n + G)
                    c_query(u % 2, n + 2)

            with pool.Fori(0, T - 1) as i:
                for u in range(SPT):
                    c_step(i, u, False)
            for u in range(SPT):
                c_step(T - 1, u, True)
            pool.wait_ge(c_x, T)
            pool.wait_ge(consts_made, 2)
            pool.wait_ge(pl_scale_ready, 2)

            def lines(l, m):
                p1, p2 = pp[l][:, 0], pp[l][:, 1]
                pool.wait_ge(s["lines_in"], tile(m, l))
                pairs = ((0, 0, 1, 3), (3, 1, 2, 2), (5, 2, 3, 1))
                for dst, u, w in ((la[l], p1, p2), (lb[l], p2, p1)):
                    for at, pi, pj, k in pairs:
                        r = p.tensor_tensor(dst[:, :, at:at + k], u[:, :, pi:pi + 1].broadcast_to([P, H, k]),
                                            w[:, :, pj:pj + k], ALU.mult)
                r.then_inc(s["lines_mul"], 1)
                pool.wait_ge(s["lines_mul"], 2 * (NL * m + l) + 1)
                p.tensor_tensor(la[l][:, :, :], la[l][:, :, :], lb[l][:, :, :], ALU.subtract).then_inc(s["lines_mul"], 1)
                pool.wait_ge(s["lines_mul"], 2 * (NL * m + l) + 2)
                p.tensor_tensor(lb[l][:, :, :], la[l][:, :, :], la[l][:, :, :], ALU.mult).then_inc(s["lines_sq"], 1)

            def lines_unit(l, m):
                pool.wait_ge(s["lines_sum"], 2 * (NL * m + l) + 2)
                p.tensor_tensor(lrn[l][:, :], lsq[l][:, :], minus_half[:, :], ALU.pow).then_inc(s["lines_step"], 1)
                pool.wait_ge(s["lines_step"], 2 * (NL * m + l) + 1)
                pool.wait_ge(s["q_evac"], tile(NT + m, l))
                p.tensor_tensor(la[l][:, :, :], la[l][:, :, :], lrn[l][:, :].unsqueeze(2).broadcast_to([P, H, NLINE]),
                                ALU.mult).then_inc(s["lines_step"], 1)
                pool.wait_ge(s["lines_step"], 2 * (NL * m + l) + 2)
                stand(pool, "pool")
                p.tensor_copy(qs[l][:, :, HD:HD + NLINE], la[l][:, :, :]).then_inc(s["q_slots"], 1)
                p.tensor_tensor(ks[l][:, :, HD:HD + NLINE], la[l][:, :, ::-1], plsc[:, :, :], ALU.mult)\
                    .then_inc(s["k_slots"], 1)

            run_lanes(pool, SLOTS1, [attention(A1, [
                (0, b_rsqrt), (2, b_bias), (4, lambda kind, l, i: lines(l, i)),
                (6, lambda kind, l, i: lines_unit(l, i))])])
            for l in range(NL):
                pool.wait_ge(s["x_updated"], tile(3 * NT - 1, l))

            def g_rsqrt(b):
                pool.wait_ge(g_mvd, TPB * b + TPB)
                stand(pool, "pool")
                p.tensor_scalar(g_ve[:, :], g_mv[:, :, 1], EPS, None, ALU.add).then_inc(g_ved, 1)
                pool.wait_ge(g_ved, b + 1)
                p.tensor_tensor(g_rstd[:, :], g_ve[:, :], minus_half[:, 0:TPB], ALU.pow).then_inc(g_rs, 1)

            with pool.Fori(0, NB) as b:
                g_rsqrt(b)


def kernel(**inputs):
    import numpy as np
    import concourse.bacc as bacc
    from concourse.bass_utils import run_bass_kernel_spmd

    a = {k: np.asarray(v) for k, v in inputs.items()}

    def cols(w):
        return np.ascontiguousarray(w.reshape(-1, P, w.shape[1]).transpose(1, 0, 2))

    def over(v):
        return np.ascontiguousarray(np.broadcast_to(v.reshape(1, -1), (P, v.size)))

    def rows(w):
        o, i = w.shape
        return np.ascontiguousarray(w.reshape(o // P, P, i).transpose(1, 0, 2).reshape(P, 48, 32))

    def feat(v):
        return v.reshape(KI, P).T

    ctxt = a["ctx_1024"]
    parts = np.arange(P)
    q = np.arange(L)
    delta = q[:, None] - q[None, :]
    visible = delta >= 0
    causal = np.where(visible, 0.0, -1e30).astype(np.float32)
    causal = np.broadcast_to(causal[None, :, None, :], (J, L, H, L)).reshape(P, H * L)
    pb = a["L0_attn_pos_bias"][np.where(visible, delta, 0)]
    pb = pb.reshape(L, L, G, J).transpose(3, 0, 2, 1)
    pb = np.broadcast_to(pb[:, :, :, None, :], (J, L, G, SPT, L)).reshape(P, H * L)
    bqkv0, bqkv1 = a["L0_attn_bqkv"], a["L1_attn_bqkv"]
    arrays = {
        "x": a["x"].reshape(T, P, D).transpose(1, 0, 2),
        "ident": np.eye(P, dtype=np.float32),
        "sel": (parts[:, None] % L == np.arange(L)).astype(np.float32),
        "mask8": (parts[:, None] // HD == np.arange(8)).astype(np.float32),
        "mask4": (parts[:, None] // L == np.arange(4)).astype(np.float32),
        "causal": causal,
        "posbias": pb,
        "colb": np.stack([feat(v) for v in (
            a["L0_xattn_bq"], a["L0_xattn_bk"], a["L0_xattn_bv"], bqkv0[0:D], bqkv0[D:2 * D], bqkv0[2 * D:],
            a["L0_attn_bgate"], a["L1_xattn_bq"], a["L1_xattn_bk"], a["L1_xattn_bv"])], axis=1),
        "rowb": np.stack([over(a[k]) for k in ("L0_xattn_bo", "L0_attn_bout", "L1_xattn_bo", "L1_attn_bout")],
                         axis=1),
        "a1_bv": feat(bqkv1[2 * D:]),
        "a1_bqk": over(bqkv1[0:2 * D]),
        "plscale": over(a["L1_attn_plucker_scale"]),
        "plsign": over(np.array([1, -1, 1, 1, -1, 1], np.float32)),
        "x0_wq": cols(a["L0_xattn_Wq"].T), "x0_wk": cols(a["L0_xattn_Wk"].T),
        "x0_wv": cols(a["L0_xattn_Wv"].T), "x0_wo": cols(a["L0_xattn_Wo"].T),
        "a0_wqkv": cols(a["L0_attn_Wqkv"]), "a0_wg": cols(a["L0_attn_Wgate"]), "a0_wout": cols(a["L0_attn_Wout"]),
        "w_up": rows(a["L0_ffn_w_up"]), "w_gate": rows(a["L0_ffn_w_gate"]), "w_down": rows(a["L0_ffn_w_down"]),
        "x1_wq": cols(a["L1_xattn_Wq"].T), "x1_wk": cols(a["L1_xattn_Wk"].T),
        "x1_wv": cols(a["L1_xattn_Wv"].T), "x1_wo": cols(a["L1_xattn_Wo"].T),
        "a1_wqkv": cols(a["L1_attn_Wqkv"]), "a1_wout": cols(a["L1_attn_Wout"]),
        "a1_wpl": np.stack([cols(a["L1_attn_W1p"]), cols(a["L1_attn_W2p"])], axis=2),
        "f_w1": cols(a["L1_ffn_w1_w"].T), "f_w2": cols(a["L1_ffn_w2_w"].T), "f_h1": cols(a["L1_ffn_h1_w"].T),
        "f_h2": cols(a["L1_ffn_h2_w"].T), "f_w3": cols(a["L1_ffn_w3_w"].T),
        "ffn_s": np.stack([a[f"L1_ffn_{k}_s"].reshape(NF1, P).T for k in ("w1", "w2", "h1", "h2")], axis=1),
        "w3s": over(a["L1_ffn_w3_s"]),
        "ctxT": ctxt.reshape(NSEQ, S, KI, P).transpose(0, 3, 2, 1),
        "ctx_last": ctxt[:, S - 1, :].reshape(NSEQ, KI, P).transpose(2, 1, 0),
        "ctxk": ctxt[:, 0:L, :].reshape(T, P, KI, P).transpose(3, 0, 2, 1),
    }
    arrays = {k: np.ascontiguousarray(v) for k, v in arrays.items()}
    nc = bacc.Bacc("TRN2", target_bir_lowering=False, num_devices=1)
    A = {k: nc.dram_tensor(f"in_{k}", v.shape, F32, kind="ExternalInput").ap() for k, v in arrays.items()}
    out = nc.dram_tensor("out", (P, T, D), F32, kind="ExternalOutput").ap()
    perceiver(nc, A, out)
    r = run_bass_kernel_spmd(nc, [{f"in_{k}": v for k, v in arrays.items()}], core_ids=[0])
    got = np.asarray(r.results[0]["out"])
    return np.ascontiguousarray(got.transpose(1, 0, 2)).reshape(NSEQ, L, D)
```
